# Optimizing a Trainium2 kernel written in Bass

```python
import numpy as np
import jax
import jax.numpy as jnp

def _softmax(x, axis=-1):
    return jax.nn.softmax(x, axis=axis)

def _gelu(x):
    return jax.nn.gelu(x, approximate=True)

def _silu(x):
    return jax.nn.silu(x)

def _sigmoid(x):
    return jax.nn.sigmoid(x)

def _layernorm(x, axis=-1, eps=1e-05):
    m = jnp.mean(x, axis=axis, keepdims=True)
    v = jnp.var(x, axis=axis, keepdims=True)
    return (x - m) / jnp.sqrt(v + eps)

def _scatter_add(tgt, idx, src, axis=0):
    return tgt.at[idx].add(src)

def _segment_sum(src, seg, n):
    return jax.ops.segment_sum(src, seg, n)
kernel_name = 'mk_xattn_seq_d2_seqx_r8_9a1179'

def setup_inputs(seed: int=0):
    np.random.seed(seed)
    _w = jnp.asarray

    def _rec_inputs():
        import jax
        import jax.numpy as jnp
        _rk = jax.random.key(seed)
        x = -0.0003929 + 0.9999 * jax.random.normal(jax.random.fold_in(_rk, 1), (4, 256, 256), jnp.float32)
        _lenS = 256 - jax.random.randint(jax.random.fold_in(_rk, 7), (4,), 0, max(1, 256 // 4) + 1, jnp.int32)
        _lenS2 = 1601 - jax.random.randint(jax.random.fold_in(_rk, 8), (4,), 0, max(1, 1601 // 4) + 1, jnp.int32)
        _ctx_1024P = jax.random.normal(jax.random.fold_in(_rk, 11), (4, 16, 128), jnp.float32)
        _ctx_1024c = jax.random.dirichlet(jax.random.fold_in(_rk, 511), 0.3 * jnp.ones((16,), jnp.float32), (4, 1601))
        _ctx_1024t = jnp.einsum('bsk,bkd->bsd', _ctx_1024c, _ctx_1024P)
        _ctx_1024t = _ctx_1024t * jax.lax.rsqrt(jnp.mean(jnp.square(_ctx_1024t)) + 1e-12) * 0.953939
        ctx_1024 = 0.00191187 + 0.999416 * (_ctx_1024t + 0.3 * jax.random.normal(jax.random.fold_in(_rk, 611), (4, 1601, 128), jnp.float32))
        _validS = jnp.arange(256)[None, :] < _lenS[:, None]
        _validS2 = jnp.arange(1601)[None, :] < _lenS2[:, None]
        _causal = jnp.tril(jnp.ones((256, 256), dtype=bool))
        mask_BxS2_bk0 = jnp.logical_not(jnp.broadcast_to(_validS2[:, :], (4, 1601)))
        return (x, ctx_1024, mask_BxS2_bk0)
    x, ctx_1024, mask_BxS2_bk0 = _rec_inputs()

    def _L0_xattn_setup():
        import jax, jax.numpy as jnp
        import numpy as np
        DIM = 256
        DIM_MEDIA = 128
        HEADS = 16
        DIM_HEAD = 64
        INNER = HEADS * DIM_HEAD
        FF_INNER = 4 * DIM
        B, N_TOK, N_LAT = (4, 256, 64)
        EPS = 1e-05

        def layernorm(x, g, b):
            mu = jnp.mean(x, axis=-1, keepdims=True)
            var = jnp.var(x, axis=-1, keepdims=True)
            return (x - mu) * jax.lax.rsqrt(var + EPS) * g + b
        key = jax.random.key(seed)
        ks = jax.random.split(key, 12)
        x = jax.random.normal(ks[0], (B, N_TOK, DIM), dtype=jnp.float32)
        media = jax.random.normal(ks[1], (B, N_LAT, DIM_MEDIA), dtype=jnp.float32)
        media_mask = jax.random.randint(ks[2], (B, N_LAT), 0, 2).astype(bool)
        media_mask = media_mask.at[:, 0].set(True)
        s = lambda d: 1.0 / np.sqrt(d)
        Wq = jax.random.normal(ks[3], (DIM, INNER), dtype=jnp.float32) * s(DIM)
        Wkv = jax.random.normal(ks[4], (DIM_MEDIA, 2 * INNER), dtype=jnp.float32) * s(DIM_MEDIA)
        Wo = jax.random.normal(ks[5], (INNER, DIM), dtype=jnp.float32) * s(INNER)
        W1 = jax.random.normal(ks[6], (DIM, FF_INNER), dtype=jnp.float32) * s(DIM)
        W2 = jax.random.normal(ks[7], (FF_INNER, DIM), dtype=jnp.float32) * s(FF_INNER)
        return {'x': x, 'media': media, 'media_mask': media_mask, 'ln_q_g': jnp.ones((DIM,), jnp.float32), 'ln_q_b': jnp.zeros((DIM,), jnp.float32), 'Wq': Wq, 'Wkv': Wkv, 'Wo': Wo, 'attn_gate': jax.random.normal(ks[8], (1,), jnp.float32) * 0.5, 'ln_ff_g': jnp.ones((DIM,), jnp.float32), 'ln_ff_b': jnp.zeros((DIM,), jnp.float32), 'W1': W1, 'W2': W2, 'ff_gate': jax.random.normal(ks[9], (1,), jnp.float32) * 0.5}
    _L0_xattn_all = _L0_xattn_setup()
    _L0_xattn_in = {k: v for k, v in _L0_xattn_all.items() if k in ('ln_q_g', 'ln_q_b', 'Wq', 'Wkv', 'Wo', 'attn_gate', 'ln_ff_g', 'ln_ff_b', 'W1', 'W2', 'ff_gate')}
    del _L0_xattn_all

    def _L1_xattn_setup():
        import jax, jax.numpy as jnp
        import numpy as np
        EPS = 1e-06

        def _rmsnorm(x, w):
            var = jnp.mean(jnp.square(x), axis=-1, keepdims=True)
            return x * jax.lax.rsqrt(var + EPS) * w
        key = jax.random.key(seed)
        ks = jax.random.split(key, 6)
        B, N, M = (4, 512, 256)
        d_model, memory_dim = (256, 128)
        hidden_states = jax.random.normal(ks[0], (B, N, d_model), dtype=jnp.float32)
        memory = jax.random.normal(ks[1], (B, M, memory_dim), dtype=jnp.float32)
        W_mem = jax.random.normal(ks[2], (d_model, memory_dim), dtype=jnp.float32) / np.sqrt(memory_dim)
        W_gate = jax.random.normal(ks[3], (d_model, 2 * d_model), dtype=jnp.float32) / np.sqrt(2 * d_model)
        b_gate = jax.random.normal(ks[4], (d_model,), dtype=jnp.float32) * 0.01
        norm_w = jnp.ones((d_model,), dtype=jnp.float32)
        return {'hidden_states': hidden_states, 'memory': memory, 'W_mem': W_mem, 'W_gate': W_gate, 'b_gate': b_gate, 'norm_w': norm_w}
    _L1_xattn_all = _L1_xattn_setup()
    _L1_xattn_in = {k: v for k, v in _L1_xattn_all.items() if k in ('W_mem', 'W_gate', 'b_gate', 'norm_w')}
    del _L1_xattn_all
    return {'x': x, 'ctx_1024': ctx_1024, 'mask_BxS2_bk0': mask_BxS2_bk0, 'L0_xattn_ln_q_g': _L0_xattn_in['ln_q_g'], 'L0_xattn_ln_q_b': _L0_xattn_in['ln_q_b'], 'L0_xattn_Wq': _L0_xattn_in['Wq'], 'L0_xattn_Wkv': _L0_xattn_in['Wkv'], 'L0_xattn_Wo': _L0_xattn_in['Wo'], 'L0_xattn_attn_gate': _L0_xattn_in['attn_gate'], 'L0_xattn_ln_ff_g': _L0_xattn_in['ln_ff_g'], 'L0_xattn_ln_ff_b': _L0_xattn_in['ln_ff_b'], 'L0_xattn_W1': _L0_xattn_in['W1'], 'L0_xattn_W2': _L0_xattn_in['W2'], 'L0_xattn_ff_gate': _L0_xattn_in['ff_gate'], 'L1_xattn_W_mem': _L1_xattn_in['W_mem'], 'L1_xattn_W_gate': _L1_xattn_in['W_gate'], 'L1_xattn_b_gate': _L1_xattn_in['b_gate'], 'L1_xattn_norm_w': _L1_xattn_in['norm_w']}

def reference(x, ctx_1024, mask_BxS2_bk0, L0_xattn_ln_q_g, L0_xattn_ln_q_b, L0_xattn_Wq, L0_xattn_Wkv, L0_xattn_Wo, L0_xattn_attn_gate, L0_xattn_ln_ff_g, L0_xattn_ln_ff_b, L0_xattn_W1, L0_xattn_W2, L0_xattn_ff_gate, L1_xattn_W_mem, L1_xattn_W_gate, L1_xattn_b_gate, L1_xattn_norm_w):
    import jax
    import jax.numpy as jnp

    def _L0_xattn_ref(x, media, media_mask, ln_q_g, ln_q_b, Wq, Wkv, Wo, attn_gate, ln_ff_g, ln_ff_b, W1, W2, ff_gate):
        import jax, jax.numpy as jnp
        import numpy as np
        DIM = 256
        DIM_MEDIA = 128
        HEADS = 16
        DIM_HEAD = 64
        INNER = HEADS * DIM_HEAD
        FF_INNER = 4 * DIM
        B, N_TOK, N_LAT = (4, 256, 64)
        EPS = 1e-05

        def layernorm(x, g, b):
            mu = jnp.mean(x, axis=-1, keepdims=True)
            var = jnp.var(x, axis=-1, keepdims=True)
            return (x - mu) * jax.lax.rsqrt(var + EPS) * g + b
        scale = DIM_HEAD ** (-0.5)
        qn = layernorm(x, ln_q_g, ln_q_b)
        q = qn @ Wq * scale
        kv = media @ Wkv
        k, v = jnp.split(kv, 2, axis=-1)
        split_heads = lambda t: t.reshape(t.shape[0], t.shape[1], HEADS, DIM_HEAD).transpose(0, 2, 1, 3)
        q, k, v = (split_heads(q), split_heads(k), split_heads(v))
        sim = jnp.einsum('bhid,bhjd->bhij', q, k)
        neg_inf = jnp.finfo(sim.dtype).min
        sim = jnp.where(media_mask[:, None, None, :], sim, neg_inf)
        attn = jax.nn.softmax(sim, axis=-1)
        out = jnp.einsum('bhij,bhjd->bhid', attn, v)
        out = out.transpose(0, 2, 1, 3).reshape(x.shape[0], x.shape[1], INNER)
        attn_out = out @ Wo
        x = x + jnp.tanh(attn_gate) * attn_out
        h = layernorm(x, ln_ff_g, ln_ff_b)
        h = jax.nn.gelu(h @ W1, approximate=False) @ W2
        x = x + jnp.tanh(ff_gate) * h
        return x

    def _L1_xattn_ref(hidden_states, memory, W_mem, W_gate, b_gate, norm_w):
        import jax, jax.numpy as jnp
        import numpy as np
        EPS = 1e-06

        def _rmsnorm(x, w):
            var = jnp.mean(jnp.square(x), axis=-1, keepdims=True)
            return x * jax.lax.rsqrt(var + EPS) * w
        D = hidden_states.shape[-1]
        memory_proj = jnp.einsum('bme,de->bmd', memory, W_mem)
        scores = jnp.einsum('bnd,bmd->bnm', hidden_states, memory_proj) / jnp.sqrt(jnp.float32(D))
        attn = jax.nn.softmax(scores, axis=-1)
        memory_context = jnp.einsum('bnm,bmd->bnd', attn, memory_proj)
        gate_input = jnp.concatenate([hidden_states, memory_context], axis=-1)
        gate = jax.nn.sigmoid(jnp.einsum('bnf,df->bnd', gate_input, W_gate) + b_gate)
        fused = hidden_states + gate * memory_context
        return _rmsnorm(fused, norm_w)
    x = _L0_xattn_ref(x, ctx_1024, mask_BxS2_bk0, L0_xattn_ln_q_g, L0_xattn_ln_q_b, L0_xattn_Wq, L0_xattn_Wkv, L0_xattn_Wo, L0_xattn_attn_gate, L0_xattn_ln_ff_g, L0_xattn_ln_ff_b, L0_xattn_W1, L0_xattn_W2, L0_xattn_ff_gate)
    x = _L1_xattn_ref(x, ctx_1024, L1_xattn_W_mem, L1_xattn_W_gate, L1_xattn_b_gate, L1_xattn_norm_w)
    return x

_drawn_inputs = setup_inputs


def setup_inputs(seed=0):
    import zlib

    import numpy as np

    out = dict(_drawn_inputs(seed))
    spreads = {'L0_xattn_ln_q_g': (1.0, 0.6),
     'L0_xattn_ln_q_b': (0.0, 0.8),
     'L0_xattn_ln_ff_g': (1.0, 0.6),
     'L0_xattn_ln_ff_b': (0.0, 2.0),
     'L1_xattn_norm_w': (1.0, 0.2)}
    factors = {'L1_xattn_b_gate': 52.029}
    for name, (base, spread) in spreads.items():
        noise = np.random.default_rng([zlib.crc32(name.encode()), seed]).standard_normal(out[name].shape)
        drawn = base * np.exp(spread * noise) if base else spread * noise
        out[name] = jnp.asarray(drawn.astype(out[name].dtype))
    for name, factor in factors.items():
        out[name] = (out[name] * factor).astype(out[name].dtype)
    return out
```

```python
import concourse.bass as bass
from concourse import mybir
from contextlib import ExitStack

F32 = mybir.dt.float32
F32R = mybir.dt.float32r
U8 = mybir.dt.uint8
ACT = mybir.ActivationFunctionType
ALU = mybir.AluOpType
AX = mybir.AxisListType

P = 128
BIG = 2.0 ** 100
PAIR_LOOKAHEAD = 1


def attention_order(pairs, groups, value_units, key_chunks, max_chunks):
    def keys(j):
        return [("Q", j)] + [("K", j, c) for c in range(key_chunks)]

    def maxima(j):
        return [("M", j, h, t, c) for c in range(max_chunks) for h in range(2) for t in range(2)] + [("N", j)]

    order = keys(0) + [("V", 0, u) for u in range(value_units)] + maxima(0) + [("R", 0)]
    for j in range(pairs):
        side = []
        if j + 1 < pairs:
            side = keys(j + 1) + maxima(j + 1)
            units = [("V", j // 2 + 1, u) for u in range(value_units)] if j // 2 + 1 < pairs // 2 else []
            half = (value_units + 1) // 2
            side += units[:half] if j % 2 == 0 else units[half:]
            side += [("R", j + 1)]
        share = -(-len(side) // groups)
        for g in range(groups):
            order.append(("S", j, g))
            order += side[g * share:(g + 1) * share]
            if g >= 1:
                order.append(("A", j, g - 1))
            elif j >= 1:
                order.append(("A", j - 1, groups - 1))
            if g == 2 and j >= 1:
                order.append(("D", j - 1))
    order += [("A", pairs - 1, groups - 1), ("D", pairs - 1)]
    return order


def cross_attention_kernel(nc, x, media, media_mask, ln_q_g, ln_q_b, Wq, Wkv, Wo, attn_gate,
                           ln_ff_g, ln_ff_b, W1, W2, ff_gate, W_mem, W_gate, b_gate, norm_w, out):
    BATCH, TOK, DIM = x.shape
    KEYS, MED = media.shape[1:]
    INNER = Wq.shape[1]
    FF = W1.shape[1]
    HD = 64
    PAIRS = INNER // (2 * HD)
    QT = TOK // P
    DT = DIM // P
    FT = FF // P
    KT = -(-KEYS // P)
    TAIL = KEYS - (KT - 1) * P
    GROUPS = -(-KT // 2)
    KPAD = KEYS + KEYS % 2
    assert QT == 2 and DT == 2 and MED == P and TOK == 256 and KT % 2 == 1
    CHUNKS = [(0, 402), (402, 802), (802, 1202), (1202, KPAD)]
    NCH = len(CHUNKS)
    PRING = 4
    LN_EPS, RMS_EPS = 1e-5, 1e-6
    Q_SCALE = HD ** -0.5
    L1_SCALE = float(DIM) ** -0.5
    MASK_ROW, ONE_ROW, KX = 64, 96, 97

    ORDER = attention_order(PAIRS, GROUPS, GROUPS, NCH, NCH)
    NG = PAIRS * GROUPS
    AUX = [i for i in ORDER if i[0] in "KVMR"]
    AUX_AT = {item: n for n, item in enumerate(AUX)}
    BY_ACT = [i for i in AUX if i[0] in "VR"]
    BY_DVE = [i for i in AUX if i[0] in "KM"]
    EMPTIED = {item: n + 1 for some in (BY_ACT, BY_DVE) for n, item in enumerate(some)}
    assert len(AUX) % 2 == 0

    def acc_count(n):
        j, g = divmod(n, GROUPS)
        return j * GROUPS + (1 if g <= 1 else g if g < GROUPS - 1 else GROUPS)

    x_v = x.rearrange("b (t p) d -> b p t d", p=P)
    out_v = out.rearrange("b (t p) d -> b p t d", p=P)
    media_full = media[:, 0:(KT - 1) * P, :].rearrange("b (t p) e -> b p t e", p=P)
    media_tail = media[:, (KT - 1) * P:KEYS, :]

    with ExitStack() as ctx:
        def sb(name, shape, dt=F32):
            return ctx.enter_context(nc.sbuf_tensor(name, shape, dt))

        def sem(name):
            return ctx.enter_context(nc.semaphore(name))

        ident = sb("ident", [P, P])
        ones = sb("ones", [P, P])
        mhalf = sb("mhalf", [P, QT])
        wk_hi, wk_lo = sb("wk_hi", [P, INNER], F32R), sb("wk_lo", [P, INNER], F32R)
        wv_hi, wv_lo = sb("wv_hi", [P, INNER], F32R), sb("wv_lo", [P, INNER], F32R)
        wo = sb("wo", [P, PAIRS, DIM])
        w1 = sb("w1", [P, DT, FF])
        w2 = sb("w2", [P, FT, DIM])
        wg = sb("wg", [P, 2 * DT, DIM])
        wm = sb("wm", [P, DT, MED])
        wmt = sb("wmt", [MED, DIM])
        norms = sb("norms", [P, 4, DT])
        normrows = sb("normrows", [4 * DT, P])
        normw = sb("normw", [P, DIM])
        bgate = sb("bgate", [1, DIM])
        gates = sb("gates", [P, 2])
        xs = sb("xs", [P, QT, DIM])
        nat = sb("nat", [P, KT, MED])
        mt_hi, mt_lo = sb("mt_hi", [MED, KPAD], F32R), sb("mt_lo", [MED, KPAD], F32R)
        mask8 = sb("mask8", [P, KEYS], U8)
        stat = sb("stat", [P, QT, 6])
        mv = sb("mv", [P, QT, 2])
        var = sb("var", [P, QT])
        rstd = sb("rstd", [P, QT])
        msum = sb("msum", [P, 4])
        qs = sb("qs", [P, 1])
        zt = sb("zt", [P, DT, TOK])
        qf = sb("qf", [P, PAIRS, TOK])
        gt = qf
        ot = sb("ot", [P, PAIRS, TOK])
        wq = ot[:, :, :].rearrange("p (t h) n -> p t (h n)", t=DT)
        kk = sb("kk", [P, 2, 2, 2, KPAD], F32R)
        qh = sb("qh", [P, 2, 2 * TOK], F32R)
        qm = sb("qm", [KX, 2 * TOK], F32R)
        ql = sb("ql", [KX, 2, 2 * TOK], F32R)
        vbuf = sb("vbuf", [P, 2 * KT * 2 * P])
        v = vbuf[:, :].rearrange("p (s t n) -> p s t n", s=2, t=KT)
        p1 = vbuf[:, 0:QT * KPAD].rearrange("p (t k) -> p t k", t=QT)
        pt = vbuf[:, QT * KPAD:QT * KPAD + KT * TOK].rearrange("p (t q) -> p t q", t=KT)
        pe_ring = sb("p_ring", [P, PRING, 1024])
        stage = pe_ring[:, :, :].rearrange("p a b -> p (a b)")
        raw_kv = stage[:, 0:2 * INNER]
        raw_wg = stage[:, 2 * INNER:2 * INNER + DT * 2 * DIM].rearrange("p (t n) -> p t n", t=DT)
        gm_hi, gm_lo = sb("gm_hi", [MED, TOK], F32R), sb("gm_lo", [MED, TOK], F32R)
        ut = stage[:, 0:TOK]
        cx = stage[:, 256:768].rearrange("p (t d) -> p t d", t=QT)
        ct = stage[:, 768:1280].rearrange("p (t q) -> p t q", t=DT)
        gate = stage[:, 1280:1792].rearrange("p (t d) -> p t d", t=QT)
        fused = stage[:, 1792:2304].rearrange("p (t d) -> p t d", t=QT)
        square = stage[:, 2304:2816].rearrange("p (t d) -> p t d", t=QT)
        z = stage[:, 2816:3328].rearrange("p (t d) -> p t d", t=QT)
        res = sb("res", [P, QT, DIM])
        acc = sb("acc", [P, 1024])
        mx = sb("mx", [P, 4, NCH])
        m4 = sb("m4", [P, 4])
        negm = sb("negm", [P, 4])
        rec = sb("rec", [P, TOK])
        l1max = sb("l1max", [P, QT])
        l1den = sb("l1den", [P, QT])
        l1rec = sb("l1rec", [P, QT])
        l1sum = sb("l1sum", [P, QT])

        scores = ctx.enter_context(nc.psum_tensor("scores", [P, 2048], F32))
        o_bank = [ctx.enter_context(nc.psum_tensor(f"o_bank{i}", [P, 512], F32)) for i in range(2)]
        aux = [ctx.enter_context(nc.psum_tensor(f"aux{i}", [P, 512], F32)) for i in range(2)]

        NAMES = """weights_in kv_in consts identity kv_hi kv_split wmt_psum wmt_ready
            x_in media_in mask_in mask_rows wq_in mask_row_ready q_scale_ready q_scale_psum q_scale_in
            var_ready rstd_ready z_ready zt_psum zt_ready media_t_psum media_hi media_lo q_psum qf_ready
            q_hi q_ready aux_full act_aux dve_aux k_hi m4_ready negm_ready s_full p_ready av_done acc_done
            den_full rec_ready norm_done attn_proj x1_ready ff1_psum gelu_ready ff2_psum x2_ready gm_psum
            gm_hi_ready gm_lo_ready l1_scores l1_max l1_exp pt_psum pt_act pt_dve u_psum u_ready ctx_psum ctx_ready
            ct_psum ct_ready gate_psum gate_ready fused_ready square_ready out_ready out_stored dve_step
            gates_ready""".split()
        S = {n: sem("s_" + n) for n in NAMES}
        DVE_STEPS = 13

        START = {"fused_ready": 1, "u_psum": 1, "attn_proj": 1, "mask_rows": 16, "out_stored": 16,
                 "den_full": 1, "norm_done": 1}

        def need(eng, name, b, per, k):
            eng.wait_ge(S[name], b * per + (k + START.get(name, 0)))

        def split_mm(dst, parts, last):
            for n, (a, m) in enumerate(parts):
                mm = nc.tensor.matmul(dst, a, m, start=(n == 0), stop=(n == len(parts) - 1))
            return mm

        def rows_of(t):
            return P if t < KT - 1 else TAIL

        block = ctx.enter_context(nc.Block())

        @block.sync
        def _(sp):
            for name, value in START.items():
                sp.sem_inc(S[name], value)
            sp.dma_start(raw_kv, Wkv).then_inc(S["kv_in"], 16)
            for dst, src in (
                (wo[:, :, :], Wo.rearrange("(t p) n -> p t n", p=P)),
                (w1[:, :, :], W1.rearrange("(t p) n -> p t n", p=P)),
                (w2[:, :, :], W2.rearrange("(t p) n -> p t n", p=P)),
                (raw_wg, W_gate.rearrange("(t p) n -> p t n", p=P)),
                (wm[:, :, :], W_mem.rearrange("(t p) n -> p t n", p=P)),
                (normrows[0:2, :], ln_q_g.rearrange("(t p) -> t p", p=P)),
                (normrows[2:4, :], ln_q_b.rearrange("(t p) -> t p", p=P)),
                (normrows[4:6, :], ln_ff_g.rearrange("(t p) -> t p", p=P)),
                (normrows[6:8, :], ln_ff_b.rearrange("(t p) -> t p", p=P)),
                (normw[:, :], norm_w.rearrange("(a n) -> a n", a=1).broadcast_to([P, DIM])),
                (bgate[:, :], b_gate.rearrange("(a n) -> a n", a=1)),
                (gates[:, 0:1], attn_gate.rearrange("(a n) -> a n", a=1).broadcast_to([P, 1])),
                (gates[:, 1:2], ff_gate.rearrange("(a n) -> a n", a=1).broadcast_to([P, 1])),
            ):
                sp.dma_start(dst, src).then_inc(S["weights_in"], 16)
            sp.wait_ge(S["consts"], 1)
            with sp.Fori(0, BATCH) as b:
                need(sp, "fused_ready", b, 1, 0)
                sp.dma_start(xs[:, :, :], x_v[b, :, :, :]).then_inc(S["x_in"], 16)
                sp.dma_start(mask8[MASK_ROW:MASK_ROW + 1, :], media_mask[bass.ds(b, 1), :]).then_inc(S["mask_in"], 16)
                need(sp, "u_psum", b, 1, 0)
                sp.dma_start(nat[:, 0:KT - 1, :], media_full[b, :, :, :]).then_inc(S["media_in"], 16)
                sp.dma_start(nat[0:TAIL, KT - 1, :], media_tail[b, :, :]).then_inc(S["media_in"], 16)
                need(sp, "attn_proj", b, 2, 0)
                sp.dma_start(wq, Wq.rearrange("(t p) n -> p t n", p=P)).then_inc(S["wq_in"], 16)
                need(sp, "mask_row_ready", b, 1, 1)
                for s, h in ((0, 1), (1, 0), (1, 1)):
                    sp.dma_start(kk[MASK_ROW:MASK_ROW + 1, 1, s, h, 0:KEYS].bitcast(F32),
                                 kk[MASK_ROW:MASK_ROW + 1, 1, 0, 0, 0:KEYS].bitcast(F32))\
                        .then_inc(S["mask_rows"], 16)
                need(sp, "out_ready", b, 2, 2)
                sp.dma_start(out_v[b, :, :, :], res[:, :, :]).then_inc(S["out_stored"], 16)
            sp.wait_ge(S["out_stored"], 16 * BATCH + START["out_stored"])

        @block.gpsimd
        def _(pool):
            nc.gpsimd.memset(ident[:, :], 0.0).then_inc(S["identity"], 1)
            pool.wait_ge(S["identity"], 1)
            nc.gpsimd.affine_select(out=ident[:, :], in_=ident[:, :], compare_op=ALU.not_equal, fill=1.0,
                                    base=0, pattern=[[-1, P]], channel_multiplier=1).then_inc(S["identity"], 1)
            nc.gpsimd.memset(mhalf[:, :], -0.5).then_inc(S["identity"], 1)
            pool.wait_ge(S["identity"], 3)

            def reciprocal_root(b, k):
                need(pool, "var_ready", b, 3, k + 1)
                nc.gpsimd.tensor_tensor(rstd[:, :], var[:, :], mhalf[:, :], ALU.pow).then_inc(S["rstd_ready"], 1)

            with pool.Fori(0, BATCH) as b:
                reciprocal_root(b, 0)
                for j in range(PAIRS):
                    n0 = j * GROUPS
                    need(pool, "p_ready", b, NG, n0 + 2)
                    need(pool, "den_full", b, PAIRS, j)
                    nc.gpsimd.tensor_tensor(acc[:, :], pe_ring[:, n0 % PRING, :], pe_ring[:, (n0 + 1) % PRING, :],
                                            ALU.add).then_inc(S["acc_done"], 1)
                    for g in range(2, GROUPS - 1):
                        need(pool, "p_ready", b, NG, n0 + g + 1)
                        need(pool, "acc_done", b, NG, n0 + g - 1)
                        nc.gpsimd.tensor_tensor(acc[:, :], acc[:, :], pe_ring[:, (n0 + g) % PRING, :],
                                                ALU.add).then_inc(S["acc_done"], 1)
                    need(pool, "acc_done", b, NG, n0 + GROUPS - 2)
                    nc.gpsimd.tensor_tensor(acc[:, 0:512], acc[:, 0:512], acc[:, 512:1024],
                                            ALU.add).then_inc(S["acc_done"], 1)
                    need(pool, "p_ready", b, NG, n0 + GROUPS)
                    need(pool, "acc_done", b, NG, n0 + GROUPS - 1)
                    nc.gpsimd.tensor_tensor(acc[0:TAIL, 0:512], acc[0:TAIL, 0:512],
                                            pe_ring[0:TAIL, (n0 + GROUPS - 1) % PRING, 0:512],
                                            ALU.add).then_inc(S["acc_done"], 1)
                reciprocal_root(b, 1)
                reciprocal_root(b, 2)

        @block.scalar
        def _(act):
            act.wait_ge(S["kv_in"], 16)
            nc.scalar.copy(wk_hi[:, :], raw_kv[:, 0:INNER]).then_inc(S["kv_hi"], 1)
            nc.scalar.copy(wv_hi[:, :], raw_kv[:, INNER:2 * INNER]).then_inc(S["kv_hi"], 1)
            act.wait_ge(S["weights_in"], 16 * 13)
            nc.scalar.activation(gates[:, :], gates[:, :], ACT.Tanh).then_inc(S["gates_ready"], 1)
            act.wait_ge(S["wmt_psum"], 1)
            nc.scalar.copy(wmt[:, :], aux[0][:, 0:DIM])
            nc.scalar.copy(wg[:, :, :], scores[:, 0:2 * DT * DIM].rearrange("p (f n) -> p f n", f=2 * DT))
            nc.scalar.copy(norms[:, :, :], aux[0][:, DIM:DIM + 4 * DT].rearrange("p (a t) -> p a t", a=4))\
                .then_inc(S["wmt_ready"], 1)
            with act.Fori(0, BATCH) as b:
                for half, (c0, c1) in enumerate(((0, 1024), (1024, KEYS))):
                    need(act, "media_t_psum", b, 2, half + 1)
                    nc.scalar.copy(mt_hi[:, c0:c1], scores[:, c0:c1]).then_inc(S["media_hi"], 1)
                need(act, "zt_psum", b, 3, 1)
                for t in range(DT):
                    last = nc.scalar.activation(zt[:, t, :], aux[0][:, t * TOK:(t + 1) * TOK], ACT.Identity,
                                                scale=norms[:, 0, t:t + 1], bias=norms[:, 1, t:t + 1])
                last.then_inc(S["zt_ready"], 1)
                need(act, "q_scale_in", b, 1, 1)
                for u in range(PAIRS // 2):
                    need(act, "q_psum", b, PAIRS // 2, u + 1)
                    bank = (o_bank[0], o_bank[1], aux[1], aux[0])[u]
                    nc.scalar.activation(qf[:, 2 * u:2 * u + 2, :], bank[:, :].rearrange("p (a q) -> p a q", a=2),
                                         ACT.Copy, scale=qs[:, 0:1]).then_inc(S["qf_ready"], 1)

                for item in ORDER:
                    kind, j = item[0], item[1]
                    if kind == "K":
                        c = item[2]
                        c0, c1 = CHUNKS[c]
                        need(act, "aux_full", b, len(AUX), AUX_AT[item] + 1)
                        if j >= 2 and c == 0:
                            need(act, "s_full", b, NG, (j - 1) * GROUPS)
                        for h in range(2):
                            src = aux[AUX_AT[item] % 2][h * HD:(h + 1) * HD, 0:c1 - c0]
                            last = nc.scalar.copy(kk[0:HD, :, j % 2, h, c0:c1],
                                                  src.unsqueeze(1).broadcast_to([HD, 2, c1 - c0]))
                        last.then_inc(S["k_hi"], 1)
                    elif kind == "V":
                        u = item[2]
                        need(act, "aux_full", b, len(AUX), AUX_AT[item] + 1)
                        if j >= 2 and u == 0:
                            need(act, "av_done", b, NG, (2 * j - 2) * GROUPS)
                        n = rows_of(2 * u)
                        w = 2 if 2 * u + 1 < KT else 1
                        nc.scalar.copy(v[0:n, j % 2, 2 * u:2 * u + w, :],
                                       aux[AUX_AT[item] % 2][0:n, 0:w * 256].rearrange("p (t n) -> p t n", t=w))\
                            .then_inc(S["act_aux"], 1)
                    elif kind == "R":
                        need(act, "aux_full", b, len(AUX), AUX_AT[item] + 1)
                        nc.scalar.copy(ql[ONE_ROW:ONE_ROW + 1, j % 2, :],
                                       aux[AUX_AT[item] % 2][ONE_ROW:ONE_ROW + 1, :]).then_inc(S["act_aux"], 1)
                    elif kind == "S":
                        g = item[2]
                        n = j * GROUPS + g
                        need(act, "s_full", b, NG, n + 1)
                        if n >= PRING:
                            need(act, "av_done", b, NG, n - PRING + 1)
                            need(act, "acc_done", b, NG, acc_count(n - PRING))
                        r, w = (P, 1024) if g < GROUPS - 1 else (TAIL, 512)
                        nc.scalar.activation(pe_ring[0:r, n % PRING, 0:w],
                                             scores[0:r, (n % 2) * 1024:(n % 2) * 1024 + w], ACT.Exp)\
                            .then_inc(S["p_ready"], 1)

                need(act, "zt_psum", b, 3, 2)
                for t in range(DT):
                    last = nc.scalar.activation(zt[:, t, :], aux[0][:, t * TOK:(t + 1) * TOK], ACT.Identity,
                                                scale=norms[:, 2, t:t + 1], bias=norms[:, 3, t:t + 1])
                last.then_inc(S["zt_ready"], 1)
                for half in range(2):
                    need(act, "ff1_psum", b, 2, half + 1)
                    nc.scalar.activation(gt[:, 4 * half:4 * half + 4, :],
                                         scores[:, half * 1024:(half + 1) * 1024].rearrange("p (c q) -> p c q", c=4),
                                         ACT.Gelu).then_inc(S["gelu_ready"], 1)
                need(act, "zt_psum", b, 3, 3)
                nc.scalar.copy(zt[:, :, :], aux[0][:, :].rearrange("p (t q) -> p t q", t=DT)).then_inc(S["zt_ready"], 1)
                need(act, "gm_psum", b, 1, 1)
                nc.scalar.activation(gm_hi[:, :], aux[1][:, 0:TOK], ACT.Copy, scale=L1_SCALE).then_inc(S["gm_hi_ready"], 1)
                for t in range(QT):
                    need(act, "l1_max", b, QT, t + 1)
                    nc.scalar.activation(p1[:, t, 0:KEYS], scores[:, 0:KEYS], ACT.Exp, bias=l1max[:, t:t + 1],
                                         accum_out=l1den[:, t:t + 1]).then_inc(S["l1_exp"], 1)
                for u in range(0, GROUPS, 2):
                    need(act, "pt_psum", b, GROUPS, u + 1)
                    r = rows_of(2 * u)
                    w = 2 if 2 * u + 1 < KT else 1
                    src = (aux[0], aux[1], o_bank[1])[u % 3]
                    nc.scalar.copy(pt[0:r, 2 * u:2 * u + w, :],
                                   src[0:r, 0:w * TOK].rearrange("p (t q) -> p t q", t=w)).then_inc(S["pt_act"], 1)
                need(act, "u_psum", b, 1, 1)
                nc.scalar.copy(ut, o_bank[0][:, 0:TOK]).then_inc(S["u_ready"], 1)
                need(act, "ct_psum", b, 1, 1)
                nc.scalar.copy(ct, aux[0][:, :].rearrange("p (t q) -> p t q", t=DT)).then_inc(S["ct_ready"], 1)
                need(act, "gate_psum", b, 1, 1)
                nc.scalar.activation(gate, aux[1][:, :].rearrange("p (t d) -> p t d", t=QT), ACT.Tanh,
                                     scale=0.5).then_inc(S["gate_ready"], 1)
                need(act, "fused_ready", b, 1, 1)
                for t in range(QT):
                    last = nc.scalar.activation(square[:, t, :], fused[:, t, :], ACT.Square,
                                                accum_out=l1sum[:, t:t + 1])
                last.then_inc(S["square_ready"], 1)

        @block.vector
        def _(dve):
            steps = [0]

            nc.vector.memset(ones[:, :], 1.0)
            nc.vector.memset(kk[HD:P, 1, :, :, :].bitcast(F32), 0.0)
            nc.vector.memset(qm[HD:KX, :].bitcast(F32), 0.0)
            nc.vector.memset(ql[HD:KX, :, :].bitcast(F32), 0.0)
            nc.vector.memset(mt_hi[:, KEYS:KPAD].bitcast(F32), 0.0)
            nc.vector.memset(mt_lo[:, KEYS:KPAD].bitcast(F32), 0.0).then_inc(S["dve_step"], 1)
            dve.wait_ge(S["dve_step"], 1)
            nc.vector.memset(kk[MASK_ROW:MASK_ROW + 1, 1, :, :, KEYS:KPAD].bitcast(F32), -BIG)
            nc.vector.memset(kk[ONE_ROW:ONE_ROW + 1, 1, :, :, :].bitcast(F32), 1.0)
            nc.vector.memset(qm[MASK_ROW:MASK_ROW + 1, :].bitcast(F32), 1.0)
            nc.vector.memset(ql[MASK_ROW:MASK_ROW + 1, :, :].bitcast(F32), 1.0).then_inc(S["consts"], 1)
            dve.wait_ge(S["kv_hi"], 1)
            nc.vector.tensor_tensor(wk_lo[:, :], raw_kv[:, 0:INNER], wk_hi[:, :].bitcast(F32), ALU.subtract)\
                .then_inc(S["kv_split"], 1)
            dve.wait_ge(S["kv_hi"], 2)
            nc.vector.tensor_tensor(wv_lo[:, :], raw_kv[:, INNER:2 * INNER], wv_hi[:, :].bitcast(F32), ALU.subtract)\
                .then_inc(S["kv_split"], 1)
            dve.wait_ge(S["gates_ready"], 1)
            dve.wait_ge(S["wmt_ready"], 1)

            with dve.Fori(0, BATCH) as b:
                steps[0] = 0

                def step(instruction):
                    steps[0] += 1
                    instruction.then_inc(S["dve_step"], 1)
                    dve.wait_ge(S["dve_step"], b * DVE_STEPS + steps[0] + 1)

                def row_norm(k):
                    for t in range(QT):
                        last = nc.vector.bn_stats(stat[:, t, :], xs[:, t, :])
                    step(last)
                    nc.vector.memset(var[:, :], 0.0)
                    for t in range(QT):
                        last = nc.vector.bn_aggr(mv[:, t, :], stat[:, t, :])
                    step(last)
                    nc.vector.tensor_scalar(var[:, :], mv[:, :, 1], LN_EPS, None, ALU.add).then_inc(S["var_ready"], 1)
                    need(dve, "rstd_ready", b, 3, k + 1)
                    for t in range(QT):
                        last = nc.vector.tensor_scalar(z[:, t, :], xs[:, t, :], mv[:, t, 0:1], rstd[:, t:t + 1],
                                                       ALU.subtract, ALU.mult)
                    last.then_inc(S["z_ready"], 1)

                need(dve, "x_in", b, 16, 16)
                row_norm(0)
                r = slice(MASK_ROW, MASK_ROW + 1)
                need(dve, "mask_in", b, 16, 16)
                step(nc.vector.reduce_sum(msum[r, 0:1], mask8[r, :], axis=AX.X))
                step(nc.vector.tensor_scalar(msum[r, 1:2], msum[r, 0:1], 0.5, None, ALU.is_le))
                nc.vector.tensor_scalar(msum[r, 2:3], msum[r, 1:2], -Q_SCALE, Q_SCALE, ALU.mult, ALU.add)\
                    .then_inc(S["q_scale_ready"], 1)
                step(nc.vector.tensor_scalar(msum[r, 3:4], msum[r, 1:2], -BIG, BIG, ALU.mult, ALU.add))
                need(dve, "mask_rows", b, 48, 0)
                nc.vector.tensor_scalar(kk[r, 1, 0, 0, 0:KEYS], mask8[r, :], -1.0, msum[r, 3:4], ALU.add, ALU.mult)\
                    .then_inc(S["mask_row_ready"], 1)
                need(dve, "q_scale_psum", b, 1, 1)
                nc.vector.tensor_copy(qs[:, :], aux[1][:, 0:1]).then_inc(S["q_scale_in"], 1)
                for half, (c0, c1) in enumerate(((0, 1024), (1024, KEYS))):
                    need(dve, "media_hi", b, 2, half + 1)
                    nc.vector.tensor_tensor(mt_lo[:, c0:c1], scores[:, c0:c1], mt_hi[:, c0:c1].bitcast(F32),
                                            ALU.subtract).then_inc(S["media_lo"], 1)

                for item in ORDER:
                    kind, j = item[0], item[1]
                    s = j % 2
                    if kind == "Q":
                        need(dve, "qf_ready", b, PAIRS // 2, j // 2 + 1)
                        if j >= 2:
                            need(dve, "s_full", b, NG, (j - 1) * GROUPS)
                        for h in range(2):
                            src = qf[h * HD:(h + 1) * HD, j, :]
                            cols = slice(h * TOK, (h + 1) * TOK)
                            nc.vector.tensor_copy(qh[0:HD, s, cols], src)
                            nc.vector.tensor_copy(qh[HD:P, s, cols], src)
                            last = nc.vector.tensor_copy(qm[0:HD, cols], src)
                        last.then_inc(S["q_hi"], 1)
                        need(dve, "q_hi", b, PAIRS, j + 1)
                        for h in range(2):
                            part = slice(h * HD, (h + 1) * HD)
                            cols = slice(h * TOK, (h + 1) * TOK)
                            last = nc.vector.tensor_tensor(ql[0:HD, s, cols], qf[part, j, :],
                                                           qh[part, s, cols].bitcast(F32), ALU.subtract)
                        last.then_inc(S["q_ready"], 1)
                    elif kind == "K":
                        c0, c1 = CHUNKS[item[2]]
                        need(dve, "k_hi", b, PAIRS * NCH, j * NCH + item[2] + 1)
                        for h in range(2):
                            last = nc.vector.tensor_tensor(kk[HD:P, 0, s, h, c0:c1],
                                                           aux[AUX_AT[item] % 2][h * HD:(h + 1) * HD, 0:c1 - c0],
                                                           kk[0:HD, 0, s, h, c0:c1].bitcast(F32), ALU.subtract)
                        last.then_inc(S["dve_aux"], 1)
                    elif kind == "M":
                        h, t, c = item[2:]
                        c0, c1 = CHUNKS[c]
                        need(dve, "aux_full", b, len(AUX), AUX_AT[item] + 1)
                        nc.vector.reduce_max(mx[:, 2 * h + t, c:c + 1], aux[AUX_AT[item] % 2][:, 0:c1 - c0],
                                             axis=AX.X).then_inc(S["dve_aux"], 1)
                    elif kind == "N":
                        need(dve, "dve_aux", b, len(BY_DVE), EMPTIED[("M", j, 1, 1, NCH - 1)])
                        nc.vector.tensor_reduce(m4[:, :], mx[:, :, :], axis=AX.X, op=ALU.max).then_inc(S["m4_ready"], 1)
                        need(dve, "m4_ready", b, PAIRS, j + 1)
                        nc.vector.tensor_scalar(negm[:, :], m4[:, :], -1.0, None, ALU.mult).then_inc(S["negm_ready"], 1)
                    elif kind == "D":
                        need(dve, "norm_done", b, PAIRS, j)
                        need(dve, "den_full", b, PAIRS, j + 1)
                        nc.vector.reciprocal(rec[:, :], o_bank[s][:, TOK:2 * TOK]).then_inc(S["rec_ready"], 1)
                        need(dve, "rec_ready", b, PAIRS, j + 1)
                        nc.vector.tensor_tensor(ot[:, j, :], o_bank[s][:, 0:TOK], rec[:, :], ALU.mult)\
                            .then_inc(S["norm_done"], 1)

                for t in range(QT):
                    need(dve, "attn_proj", b, QT, t + 1)
                    last = nc.vector.scalar_tensor_tensor(xs[:, t, :], o_bank[t][:, 0:DIM], gates[:, 0:1], xs[:, t, :],
                                                          ALU.mult, ALU.add)
                step(last)
                row_norm(1)
                for t in range(QT):
                    need(dve, "ff2_psum", b, QT, t + 1)
                    last = nc.vector.scalar_tensor_tensor(xs[:, t, :], o_bank[t][:, 0:DIM], gates[:, 1:2], xs[:, t, :],
                                                          ALU.mult, ALU.add)
                last.then_inc(S["x2_ready"], 1)
                need(dve, "gm_hi_ready", b, 1, 1)
                nc.vector.scalar_tensor_tensor(gm_lo[:, :], aux[1][:, 0:TOK], L1_SCALE, gm_hi[:, :].bitcast(F32),
                                               ALU.mult, ALU.subtract).then_inc(S["gm_lo_ready"], 1)
                for t in range(QT):
                    need(dve, "l1_scores", b, QT, t + 1)
                    step(nc.vector.reduce_max(m4[:, t:t + 1], scores[:, 0:KEYS], axis=AX.X))
                    nc.vector.tensor_scalar(l1max[:, t:t + 1], m4[:, t:t + 1], -1.0, None, ALU.mult)\
                        .then_inc(S["l1_max"], 1)
                for u in range(1, GROUPS, 2):
                    need(dve, "pt_psum", b, GROUPS, u + 1)
                    src = (aux[0], aux[1], o_bank[1])[u % 3]
                    nc.vector.tensor_copy(pt[:, 2 * u:2 * u + 2, :], src[:, :].rearrange("p (t q) -> p t q", t=2))\
                        .then_inc(S["pt_dve"], 1)
                need(dve, "l1_exp", b, QT, QT)
                step(nc.vector.reciprocal(l1rec[:, :], l1den[:, :]))
                need(dve, "ctx_psum", b, 1, 1)
                for t in range(QT):
                    last = nc.vector.tensor_scalar(cx[:, t, :], o_bank[1][:, t * DIM:(t + 1) * DIM], l1rec[:, t:t + 1],
                                                   None, ALU.mult)
                last.then_inc(S["ctx_ready"], 1)
                need(dve, "gate_ready", b, 1, 1)
                step(nc.vector.tensor_scalar(gate, gate, 0.5, 0.5, ALU.mult, ALU.add))
                step(nc.vector.tensor_tensor(fused, gate, cx, ALU.mult))
                nc.vector.tensor_tensor(fused, fused, xs[:, :, :], ALU.add).then_inc(S["fused_ready"], 1)
                need(dve, "square_ready", b, 1, 1)
                nc.vector.tensor_scalar(var[:, :], l1sum[:, :], 1.0 / DIM, RMS_EPS, ALU.mult, ALU.add)\
                    .then_inc(S["var_ready"], 1)
                need(dve, "rstd_ready", b, 3, 3)
                need(dve, "out_stored", b, 16, 0)
                for t in range(QT):
                    nc.vector.scalar_tensor_tensor(res[:, t, :], fused[:, t, :], rstd[:, t:t + 1], normw[:, :],
                                                   ALU.mult, ALU.mult).then_inc(S["out_ready"], 1)
            assert steps[0] == DVE_STEPS, steps[0]

        @block.tensor
        def _(pe):
            mm = nc.tensor.matmul
            pe.wait_ge(S["identity"], 3)
            pe.wait_ge(S["consts"], 1)
            pe.wait_ge(S["weights_in"], 16 * 13)
            for t in range(DT):
                last = nc.tensor.transpose(aux[0][:, t * P:(t + 1) * P], wm[:, t, :], ident[:, :])
            for f in range(2 * DT):
                for t in range(DT):
                    nc.tensor.transpose(scores[:, f * DIM + t * P:f * DIM + (t + 1) * P],
                                        raw_wg[:, t, f * P:(f + 1) * P], ident[:, :])
            last = nc.tensor.transpose(aux[0][:, DIM:DIM + 4 * DT], normrows[:, :], ident[0:4 * DT, 0:4 * DT])
            last.then_inc(S["wmt_psum"], 1)
            pe.wait_ge(S["wmt_ready"], 1)
            pe.wait_ge(S["kv_split"], 2)

            def transpose_tokens(dst, src):
                for t in range(DT):
                    for q in range(QT):
                        last = nc.tensor.transpose(dst[:, t * TOK + q * P:t * TOK + (q + 1) * P],
                                                   src[:, q, t * P:(t + 1) * P], ident[:, :])
                return last

            with pe.Fori(0, BATCH) as b:
                need(pe, "media_in", b, 32, 32)
                for t in range(KT):
                    r = rows_of(t)
                    last = nc.tensor.transpose(scores[:, t * P:t * P + r], nat[0:r, t, :], ident[0:r, 0:r])
                    if t in (7, KT - 1):
                        last.then_inc(S["media_t_psum"], 1)
                need(pe, "z_ready", b, 2, 1)
                transpose_tokens(aux[0], z).then_inc(S["zt_psum"], 1)
                need(pe, "q_scale_ready", b, 1, 1)
                mm(aux[1][:, 0:1], ones[MASK_ROW:MASK_ROW + 1, :], msum[MASK_ROW:MASK_ROW + 1, 2:3],
                   start=True, stop=True).then_inc(S["q_scale_psum"], 1)
                need(pe, "zt_ready", b, 3, 1)
                need(pe, "q_scale_in", b, 1, 1)
                need(pe, "wq_in", b, 16, 16)
                for u in range(PAIRS // 2):
                    bank = (o_bank[0], o_bank[1], aux[1], aux[0])[u]
                    for i in range(2):
                        c0 = (2 * u + i) * P
                        for t in range(DT):
                            last = mm(bank[:, i * TOK:(i + 1) * TOK], wq[:, t, c0:c0 + P], zt[:, t, :],
                                      start=(t == 0), stop=(t == DT - 1))
                    last.then_inc(S["q_psum"], 1)
                need(pe, "media_lo", b, 2, 2)
                need(pe, "qf_ready", b, PAIRS // 2, PAIRS // 2)

                for item in ORDER:
                    kind, j = item[0], item[1]
                    s = j % 2
                    if kind in "KVMR":
                        n = AUX_AT[item]
                        bank = aux[n % 2]
                        if n >= 2:
                            before = AUX[n - 2]
                            by, per = ("act_aux", len(BY_ACT)) if before in BY_ACT else ("dve_aux", len(BY_DVE))
                            need(pe, by, b, per, EMPTIED[before])
                    if kind == "K":
                        c0, c1 = CHUNKS[item[2]]
                        w = slice(j * P, (j + 1) * P)
                        split_mm(bank[:, 0:c1 - c0], [(wk_hi[:, w], mt_hi[:, c0:c1]), (wk_hi[:, w], mt_lo[:, c0:c1]),
                                                      (wk_lo[:, w], mt_hi[:, c0:c1])], None).then_inc(S["aux_full"], 1)
                    elif kind == "V":
                        w = slice(j * 256, (j + 1) * 256)
                        for i, t in enumerate(range(2 * item[2], min(2 * item[2] + 2, KT))):
                            r = rows_of(t)
                            k = slice(t * P, t * P + r)
                            last = split_mm(bank[0:r, i * 256:(i + 1) * 256],
                                            [(mt_hi[:, k], wv_hi[:, w]), (mt_hi[:, k], wv_lo[:, w]),
                                             (mt_lo[:, k], wv_hi[:, w])], None)
                        last.then_inc(S["aux_full"], 1)
                    elif kind == "M":
                        h, t, c = item[2:]
                        c0, c1 = CHUNKS[c]
                        if h == 0 and t == 0:
                            need(pe, "k_hi", b, PAIRS * NCH, j * NCH + c + 1)
                            if c == 0:
                                need(pe, "q_ready", b, PAIRS, j + 1)
                                if j == 0:
                                    need(pe, "mask_rows", b, 48, 48)
                        q0 = h * TOK + t * P
                        mm(bank[:, 0:c1 - c0], qm[:, q0:q0 + P], kk[0:KX, 1, s, h, c0:c1],
                           start=True, stop=True).then_inc(S["aux_full"], 1)
                    elif kind == "R":
                        need(pe, "negm_ready", b, PAIRS, j + 1)
                        for i in range(4):
                            last = mm(bank[ONE_ROW:ONE_ROW + 1, i * P:(i + 1) * P], negm[:, i:i + 1], ident[:, :],
                                      start=True, stop=True)
                        last.then_inc(S["aux_full"], 1)
                    elif kind == "S":
                        g = item[2]
                        n = j * GROUPS + g
                        if g == 0:
                            need(pe, "dve_aux", b, len(BY_DVE), EMPTIED[("K", j, NCH - 1)])
                            need(pe, "act_aux", b, len(BY_ACT), EMPTIED[("R", j)])
                        if n >= 2:
                            need(pe, "p_ready", b, NG, n - 1)
                        for i, t in enumerate(range(2 * g, min(2 * g + 2, KT))):
                            r = rows_of(t)
                            k = slice(t * P, t * P + r)
                            for h in range(2):
                                c0 = (n % 2) * 1024 + i * 512 + h * TOK
                                q = slice(h * TOK, (h + 1) * TOK)
                                mm(scores[0:r, c0:c0 + TOK], kk[:, 0, s, h, k], qh[:, s, q], start=True, stop=False)
                                last = mm(scores[0:r, c0:c0 + TOK], kk[0:KX, 1, s, h, k], ql[:, s, q],
                                          start=False, stop=True)
                        last.then_inc(S["s_full"], 1)
                    elif kind == "A":
                        g = item[2]
                        n = j * GROUPS + g
                        need(pe, "p_ready", b, NG, n + 1)
                        if g == 0:
                            if j >= 2:
                                need(pe, "norm_done", b, PAIRS, j - 1)
                            need(pe, "act_aux", b, len(BY_ACT), EMPTIED[("V", j // 2, GROUPS - 1)])
                        for i, t in enumerate(range(2 * g, min(2 * g + 2, KT))):
                            r = rows_of(t)
                            for h in range(2):
                                d0 = (j % 2) * P + h * HD
                                last = mm(o_bank[s][h * HD:(h + 1) * HD, 0:TOK], v[0:r, (j // 2) % 2, t, d0:d0 + HD],
                                          pe_ring[0:r, n % PRING, i * 512 + h * TOK:i * 512 + (h + 1) * TOK],
                                          start=(t == 0), stop=(t == KT - 1))
                        last.then_inc(S["av_done"], 1)
                    elif kind == "D":
                        need(pe, "acc_done", b, NG, (j + 1) * GROUPS)
                        for h in range(2):
                            last = mm(o_bank[s][h * HD:(h + 1) * HD, TOK:2 * TOK], ones[:, 0:HD],
                                      acc[:, h * TOK:(h + 1) * TOK], start=True, stop=True)
                        last.then_inc(S["den_full"], 1)

                need(pe, "norm_done", b, PAIRS, PAIRS)
                for t in range(QT):
                    for j in range(PAIRS):
                        last = mm(o_bank[t][:, 0:DIM], ot[:, j, t * P:(t + 1) * P], wo[:, j, :],
                                  start=(j == 0), stop=(j == PAIRS - 1))
                    last.then_inc(S["attn_proj"], 1)
                need(pe, "z_ready", b, 2, 2)
                transpose_tokens(aux[0], z).then_inc(S["zt_psum"], 1)
                need(pe, "zt_ready", b, 3, 2)
                for f in range(FT):
                    for t in range(DT):
                        last = mm(scores[:, f * TOK:(f + 1) * TOK], w1[:, t, f * P:(f + 1) * P], zt[:, t, :],
                                  start=(t == 0), stop=(t == DT - 1))
                    if f % 4 == 3:
                        last.then_inc(S["ff1_psum"], 1)
                for t in range(QT):
                    for f in range(FT):
                        if t == 0 and f % 4 == 0:
                            need(pe, "gelu_ready", b, 2, f // 4 + 1)
                        last = mm(o_bank[t][:, 0:DIM], gt[:, f, t * P:(t + 1) * P], w2[:, f, :],
                                  start=(f == 0), stop=(f == FT - 1))
                    last.then_inc(S["ff2_psum"], 1)
                need(pe, "x2_ready", b, 1, 1)
                transpose_tokens(aux[0], xs).then_inc(S["zt_psum"], 1)
                need(pe, "zt_ready", b, 3, 3)
                for t in range(DT):
                    last = mm(aux[1][:, 0:TOK], wm[:, t, :], zt[:, t, :], start=(t == 0), stop=(t == DT - 1))
                last.then_inc(S["gm_psum"], 1)
                need(pe, "gm_lo_ready", b, 1, 1)
                for t in range(QT):
                    if t:
                        need(pe, "l1_exp", b, QT, t)
                    q = slice(t * P, (t + 1) * P)
                    for c0 in range(0, KPAD, 512):
                        c1 = min(c0 + 512, KPAD)
                        last = split_mm(scores[:, c0:c1], [(gm_hi[:, q], mt_hi[:, c0:c1]), (gm_hi[:, q], mt_lo[:, c0:c1]),
                                                           (gm_lo[:, q], mt_hi[:, c0:c1])], None)
                    last.then_inc(S["l1_scores"], 1)
                need(pe, "l1_exp", b, QT, QT)
                for u in range(GROUPS):
                    if u >= 3:
                        w = u - 3
                        need(pe, *(("pt_dve", b, GROUPS // 2) if w % 2 else ("pt_act", b, GROUPS // 2 + 1)), w // 2 + 1)
                    bank = (aux[0], aux[1], o_bank[1])[u % 3]
                    for i, t in enumerate(range(2 * u, min(2 * u + 2, KT))):
                        r = rows_of(t)
                        for q in range(QT):
                            last = nc.tensor.transpose(bank[0:r, i * TOK + q * P:i * TOK + (q + 1) * P],
                                                       p1[:, q, t * P:t * P + r], ident[:, :])
                    last.then_inc(S["pt_psum"], 1)
                need(pe, "pt_act", b, GROUPS // 2 + 1, GROUPS // 2 + 1)
                need(pe, "pt_dve", b, GROUPS // 2, GROUPS // 2)
                for t in range(KT):
                    r = rows_of(t)
                    last = mm(o_bank[0][:, 0:TOK], nat[0:r, t, :], pt[0:r, t, :], start=(t == 0), stop=(t == KT - 1))
                last.then_inc(S["u_psum"], 1)
                need(pe, "u_ready", b, 1, 1)
                for q in range(QT):
                    last = mm(o_bank[1][:, q * DIM:(q + 1) * DIM], ut[:, q * P:(q + 1) * P], wmt[:, :],
                              start=True, stop=True)
                last.then_inc(S["ctx_psum"], 1)
                need(pe, "ctx_ready", b, 1, 1)
                transpose_tokens(aux[0], cx).then_inc(S["ct_psum"], 1)
                need(pe, "ct_ready", b, 1, 1)
                for q in range(QT):
                    dst = aux[1][:, q * DIM:(q + 1) * DIM]
                    for t in range(DT):
                        mm(dst, zt[:, t, q * P:(q + 1) * P], wg[:, t, :], start=(t == 0), stop=False)
                    for t in range(DT):
                        mm(dst, ct[:, t, q * P:(q + 1) * P], wg[:, DT + t, :], start=False, stop=False)
                    last = mm(dst, ones[0:1, :], bgate[:, :], start=False, stop=True)
                last.then_inc(S["gate_psum"], 1)


_INS = ['x', 'ctx_1024', 'mask_BxS2_bk0', 'L0_xattn_ln_q_g', 'L0_xattn_ln_q_b', 'L0_xattn_Wq', 'L0_xattn_Wkv',
        'L0_xattn_Wo', 'L0_xattn_attn_gate', 'L0_xattn_ln_ff_g', 'L0_xattn_ln_ff_b', 'L0_xattn_W1', 'L0_xattn_W2',
        'L0_xattn_ff_gate', 'L1_xattn_W_mem', 'L1_xattn_W_gate', 'L1_xattn_b_gate', 'L1_xattn_norm_w']


def kernel(**inputs):
    import numpy as _np
    import concourse.bacc as _bacc
    from concourse import mybir as _mybir
    from concourse.bass_utils import run_bass_kernel_spmd as _run

    nc = _bacc.Bacc("TRN2", target_bir_lowering=False, num_devices=1)
    arrays, args = {}, []
    for name in _INS:
        a = _np.ascontiguousarray(inputs[name])
        arrays[f"in_{name}_dram"] = a
        args.append(nc.dram_tensor(f"in_{name}_dram", a.shape, _mybir.dt.from_np(a.dtype), kind="ExternalInput").ap())
    shape = inputs['x'].shape
    args.append(nc.dram_tensor("out_0_dram", shape, _mybir.dt.float32, kind="ExternalOutput").ap())
    cross_attention_kernel(nc, *args)
    r = _run(nc, [arrays], core_ids=[0])
    return r.results[0]["out_0_dram"]
```

```python
import concourse.bass as bass
from concourse import mybir
from contextlib import ExitStack

F32 = mybir.dt.float32
F32R = mybir.dt.float32r
U8 = mybir.dt.uint8
ACT = mybir.ActivationFunctionType
ALU = mybir.AluOpType
AX = mybir.AxisListType

P = 128
BIG = 2.0 ** 100
LAG = 3
DIVIDE_AT = 4
DIVISION_FROM = 13
TOKENS_FROM = 9
RECIPROCAL_PARTS = 4


EVEN_TURN = """S0 K0 Q0 A10 Q1 A11 P0 L0 K1 S1 A12 L1 A0 M0.0.0 K2 S2 V0 A1 M0.0.1 L2 D V1 S3 P1 S4 E0 M0.1.0 M0.0.2
               M1.0.0 K3 A2 M1.1.0 A3 S5 L3 S6 M0.1.2 V2 A4 M0.1.1 M1.0.2 A5 S7 M0.0.3 M1.0.1 S8 M1.1.1 M1.1.2 S9
               M0.1.3 S10 A6 M1.0.3 M1.1.3 A7 S11 N E1 S12 E2 A8 A9 E3 R V3 F""".split()
ODD_TURN = """S0 K0 Q0 P0 S1 A10 Q1 L0 K1 A11 A12 M0.0.0 S2 L1 A0 M0.1.0 K2 S3 A1 A2 M1.0.0 L2 M0.0.1 D K3 E0 L3 S4 A3
              S5 M0.0.2 V4 V5 M1.1.0 S6 M0.1.1 M0.1.2 S7 M1.0.1 A4 M1.0.2 M0.0.3 M0.1.3 S8 A5 S9 M1.1.2 M1.0.3 A6
              M1.1.1 S10 M1.1.3 V6 S11 N E1 E2 A7 E3 A8 P1 R F S12 A9""".split()

WEIGHT = {"I": 1.5, "O": 0.0, "H": 0.5, "X": 0.5, "Y": 0.5, "B": 1.0, "C": 0.3, "Z": 0.3, "T": 0.8, "U": 0.0, "W": 0.3, "G": 0.3,
          "Q": 0.6, "P": 0.35, "K": 0.6, "L": 0.0, "V": 0.1, "M": 0.4, "N": 0.2, "R": 0.1, "E": 0.5, "F": 0.35}


def attention_order(pairs, tiles, value_units, chunks, turn_units):
    def mixed(into, some, start, step):
        into = list(into)
        for n, item in enumerate(some):
            into.insert(start + step * n, item)
        return into

    def side_work(j, values):
        values = list(values)
        some = [("K", j, 0), ("Q", j, 0)] + values[:1] + [("L", j, 0), ("Q", j, 1)] + values[1:2] + [("K", j, 1)]
        for c in range(chunks):
            m = [("M", j, h, t, c) for h in range(2) for t in range(2)]
            some += m[:2] + ([("L", j, c + 1)] if c + 1 < chunks else []) + m[2:3]
            some += ([("K", j, c + 2)] if c + 2 < chunks else []) + m[3:]
            if c >= chunks - 2:
                some.append(("P", j, c - (chunks - 2)))
        return some + [("N", j)] + values[2:3] + [("R", j)] + values[3:]

    def division(j):
        return [("E", j, i) for i in range(RECIPROCAL_PARTS)] + [("F", j)]

    tokens = [("X",), ("B",), ("Y",), ("Z",)]
    turns = [("C",), ("W", 0), ("I",), ("W", 1), ("T", 0), ("G", 0), ("T", 1), ("U", 0)]
    for u in range(2, turn_units):
        turns += [("T", u), ("U", u - 1)] + ([("G", u - 1)] if u <= pairs // 2 else [])
    turns += [("U", turn_units - 1)]
    assert sum(i[0] == "G" for i in turns) == pairs // 2
    ending = [("O", t, i) for t in range(2) for i in range(2)] + [("H",)]

    def turn(j):
        before = (0, j - 1) if j else (-1, pairs - 1)
        for word in ODD_TURN if j % 2 else EVEN_TURN:
            kind, numbers = word[0], [int(n) for n in word[1:].split(".") if n]
            if kind == "V":
                if j // 2 + 1 < pairs // 2:
                    yield (0, ("V", j // 2 + 1, *numbers))
            elif kind in "DEF" or kind == "A" and numbers[0] >= tiles - LAG:
                yield (before[0], (kind, before[1], *numbers))
            else:
                yield (0, (kind, j if kind in "SA" else j + 1, *numbers))

    order = []
    for j in range(pairs - 1):
        some = list(turn(j))
        if j == pairs - 2:
            some = mixed(some, [(1, i) for i in tokens], TOKENS_FROM, 5)
        if j == 0:
            some += [(-1, i) for i in ending]
        order += some
        if j == 0:
            head = len(order)
    for j in range(pairs - 1, pairs):
        before = (0, j - 1)
        main = []
        for t in range(tiles):
            main.append((0, ("S", j, t)))
            main.append((0, ("A", j, t - LAG)) if t >= LAG else (before[0], ("A", before[1], tiles - LAG + t)))
            if t == DIVIDE_AT:
                main.append((before[0], ("D", before[1])))
        side = [(1, i) for i in turns + side_work(0, [("V", 0, u) for u in range(value_units)])]
        late = [(before[0], i) for i in division(before[1])]
        side = mixed(side, late, DIVISION_FROM, 3)
        total, given, at = sum(WEIGHT[i[0]] for _, i in side), 0.0, 0
        for n, item in enumerate(main):
            order.append(item)
            while at < len(side) and given <= total * (n + 1) / len(main):
                if side[at][1][0] in "EF" and (before[0], ("D", before[1])) not in order:
                    break
                given += WEIGHT[side[at][1][0]]
                order.append(side[at])
                at += 1
        order += side[at:]
    return order[head:] + [(ahead + 1, item) for ahead, item in order[:head]]


def cross_attention_kernel(nc, x, media, media_mask, ln_q_g, ln_q_b, Wq, Wkv, Wo, attn_gate,
                           ln_ff_g, ln_ff_b, W1, W2, ff_gate, W_mem, W_gate, b_gate, norm_w, out):
    BATCH, TOK, DIM = x.shape
    KEYS, MED = media.shape[1:]
    INNER = Wq.shape[1]
    FF = W1.shape[1]
    HD = 64
    PAIRS = INNER // (2 * HD)
    QT = TOK // P
    DT = DIM // P
    FT = FF // P
    KT = -(-KEYS // P)
    TAIL = KEYS - (KT - 1) * P
    GROUPS = -(-KT // 2)
    KPAD = KEYS + KEYS % 2
    assert QT == 2 and DT == 2 and MED == P and TOK == 256 and KT % 2 == 1
    CHUNKS = [(0, 402), (402, 802), (802, 1202), (1202, KPAD)]
    NCH = len(CHUNKS)
    PRING = 4
    LN_EPS, RMS_EPS = 1e-5, 1e-6
    Q_SCALE = HD ** -0.5
    L1_SCALE = float(DIM) ** -0.5
    MASK_ROW, ONE_ROW, KX = 64, 96, 97

    TURN = 3
    TUNITS = -(-KT // TURN)
    NG, NT = PAIRS * GROUPS, PAIRS * KT
    SBANKS, ABANKS = 2, 4
    BODY = attention_order(PAIRS, KT, GROUPS, NCH, TUNITS)
    FIRST = [key for key in BODY if key[0] == 1]
    LAST = [key for key in BODY if key[0] == 0]

    COUNTED = {"aux_full": "KVMRTWGC", "act_aux": "VRWG", "dve_aux": "LMUC", "k_hi": "K", "t_hi": "T", "q_hi": "Q",
               "q_lo": "P", "m4_ready": "N", "negm_ready": "N", "q_scale_ready": "B", "z_ready": "Z",
               "var_ready": "X", "rstd_ready": "Y", "mask_row_ready": "I"}
    EMPTIED_BY = {"K": "L", "T": "U"}

    def counts(name, order):
        some = [x for x in order if x[1][0] in COUNTED[name]]
        return {x: n + 1 for n, x in enumerate(some)}

    IN_FIRST, IN_BODY = ({n: counts(n, order) for n in COUNTED} for order in (FIRST, BODY))

    def count(name, ahead, item):
        per, before = len(IN_BODY[name]), len(IN_FIRST[name])
        if ahead or (0, item) in IN_BODY[name]:
            return before + IN_BODY[name][(ahead, item)], per
        return before + IN_BODY[name][(1, item)] - per, per

    def aux_bank(ahead, item):
        return (count("aux_full", ahead, item)[0] - 1) % ABANKS

    AUX_BEFORE = {}
    for order in (FIRST, BODY):
        some = [key for key in ([(0, i) for _, i in FIRST] if order is BODY else []) + order
                if key[1][0] in COUNTED["aux_full"]]
        for n, key in enumerate(some):
            if n >= ABANKS and (order is FIRST or n >= len(IN_FIRST["aux_full"])):
                AUX_BEFORE[order is FIRST, key] = some[n - ABANKS]
    assert len(IN_BODY["aux_full"]) % ABANKS == 0, len(IN_BODY["aux_full"])
    assert all(IN_BODY[n][x] - len(IN_BODY[n]) + len(IN_FIRST[n]) == k
               for n in COUNTED for x, k in IN_FIRST[n].items())

    def acc_count(n):
        if n < 0:
            return acc_count(n + NG) - NG
        j, g = divmod(n, GROUPS)
        return j * GROUPS + (1 if g <= 1 else g if g < GROUPS - 1 else GROUPS)

    x_v = x.rearrange("b (t p) d -> b p t d", p=P)
    out_v = out.rearrange("b (t p) d -> b p t d", p=P)
    media_full = media[:, 0:(KT - 1) * P, :].rearrange("b (t p) e -> b p t e", p=P)
    media_tail = media[:, (KT - 1) * P:KEYS, :]

    LANES = 2
    assert BATCH % LANES == 0

    with ExitStack() as ctx:
        phase = ExitStack()

        def sb(name, shape, dt=F32):
            return ctx.enter_context(nc.sbuf_tensor(name, shape, dt))

        def ph(name, shape, dt=F32):
            return phase.enter_context(nc.sbuf_tensor(name, shape, dt))

        def sem(name):
            return ctx.enter_context(nc.semaphore(name))

        ident = sb("ident", [P, P])
        ones = sb("ones", [P, P])
        mhalf = sb("mhalf", [P, QT])
        wg = sb("wg", [P, 2 * DT, DIM])
        wm = sb("wm", [P, DT, MED])
        wmt = sb("wmt", [MED, DIM])
        norms = sb("norms", [P, 4, DT])
        bgate = sb("bgate", [1, DIM])
        gates = sb("gates", [P, 2])
        xs = sb("xs", [P, BATCH, QT, DIM])
        stat = sb("stat", [P, LANES, QT, 6])
        mv = sb("mv", [P, LANES, QT, 2])
        var = sb("var", [P, LANES, QT])
        rstd = sb("rstd", [P, LANES, QT])
        nat0 = sb("nat0", [P, KT, MED])

        kk = ph("kk", [P, 2, 2, 2, KPAD], F32R)
        wk_hi, wk_lo = ph("wk_hi", [P, INNER], F32R), ph("wk_lo", [P, INNER], F32R)
        wv_hi, wv_lo = ph("wv_hi", [P, INNER], F32R), ph("wv_lo", [P, INNER], F32R)
        wo = ph("wo", [P, PAIRS, DIM])
        wq = ph("wq", [P, DT, INNER])
        normrows = ph("normrows", [4 * DT, P])
        mt_hi, mt_lo = ph("mt_hi", [MED, KPAD], F32R), ph("mt_lo", [MED, KPAD], F32R)
        mask8 = ph("mask8", [P, KEYS], U8)
        msum = ph("msum", [P, 4])
        qs = ph("qs", [P, 1])
        z = ph("z", [P, QT, DIM])
        zt = ph("zt", [P, DT, TOK])
        qf = ph("qf", [P, PAIRS, TOK])
        ot = ph("ot", [P, PAIRS, TOK])
        qh = ph("qh", [P, 2, 2 * TOK], F32R)
        qm = ph("qm", [KX, 2 * TOK], F32R)
        ql = ph("ql", [KX, 2, 2 * TOK], F32R)
        v = ph("v", [P, 2, KT, 2 * P])
        pe_ring = ph("p_ring", [P, PRING, 1024])
        stage = pe_ring[:, :, :].rearrange("p a b -> p (a b)")
        raw_kv = stage[:, 0:2 * INNER]
        raw_wg = stage[:, 2 * INNER:2 * INNER + DT * 2 * DIM].rearrange("p (t n) -> p t n", t=DT)
        acc = ph("acc", [P, 1024])
        mx = ph("mx", [P, 4, NCH])
        m4 = ph("m4", [P, 4])
        negm = ph("negm", [P, 4])
        rec = ph("rec", [P, TOK])
        phase.close()

        w1 = ph("w1", [P, DT, FF])
        w2 = ph("w2", [P, FT, DIM])
        normw = ph("normw", [P, DIM])
        nat1 = ph("nat1", [P, KT, MED])
        nats = [nat0, nat1]

        def lanes(name, shape, dt=F32):
            return [ph(f"{name}{lane}", shape, dt) for lane in range(LANES)]

        mts_hi, mts_lo = lanes("t_mt_hi", [MED, KPAD], F32R), lanes("t_mt_lo", [MED, KPAD], F32R)
        zs = lanes("t_z", [P, QT, DIM])
        zts = lanes("t_zt", [P, DT, TOK])
        gts = lanes("t_gelu", [P, FT, TOK])
        x2s = lanes("t_x2", [P, QT, DIM])
        gms_hi, gms_lo = lanes("t_gm_hi", [MED, TOK], F32R), lanes("t_gm_lo", [MED, TOK], F32R)
        p1s = lanes("t_p1", [P, QT, KPAD])
        pts = lanes("t_pt", [P, KT, TOK])
        uts = lanes("t_u", [MED, TOK])
        cxs = lanes("t_cx", [P, QT, DIM])
        cts = lanes("t_ct", [P, DT, TOK])
        gate_s = lanes("t_gate", [P, QT, DIM])
        fuseds = lanes("t_fused", [P, QT, DIM])
        squares = lanes("t_square", [P, QT, DIM])
        ress = lanes("t_res", [P, QT, DIM])
        l1top = lanes("t_top", [P, QT])
        l1max = lanes("t_max", [P, QT])
        l1den = lanes("t_den", [P, QT])
        l1rec = lanes("t_rec", [P, QT])
        l1sum = lanes("t_sum", [P, QT])
        ctx.enter_context(phase)

        psum = ctx.enter_context(nc.psum_tensor("psum", [P, 4096], F32))
        score_bank, aux, o_bank = ([psum[:, 512 * i:512 * (i + 1)] for i in some]
                                   for some in (range(0, SBANKS), range(SBANKS, 6), range(6, 8)))
        wide = psum[:, 0:2048]
        side = [psum[:, 512 * i:512 * (i + 1)] for i in (4, 5)]
        lane_psum = [psum[:, 2048 * lane:2048 * (lane + 1)] for lane in range(LANES)]
        lane_bank = [[lane_psum[lane][:, 512 * i:512 * (i + 1)] for i in range(4)] for lane in range(LANES)]

        NAMES = """weights_in kv_in consts identity kv_hi kv_split wmt_psum wmt_ready gates_ready late_weights_in
            x_in media_in mask_in mask_rows0 mask_rows1 mask_row_ready q_scale_ready var_ready rstd_ready z_ready
            t_hi q_hi q_lo aux_full act_aux dve_aux k_hi m4_ready negm_ready s_full p_ready av_done acc_done
            den_full rec_ready norm_done attn_proj x1_ready dve_step tail_step""".split()
        LANE_NAMES = """media_in media_t_psum media_hi media_lo pad_ready var_ready rstd_ready z_ready zt_psum zt_ready
            ff1_psum gelu_ready ff2_psum x2_ready x2t_psum x2t_ready gm_psum gm_hi_ready gm_lo_ready l1_scores
            l1_max l1_exp pt_psum pt_act pt_dve u_psum u_ready ctx_psum ctx_ready ct_psum ct_ready gate_psum
            gate_ready fused_ready square_ready ssq_ready rms_ready out_ready out_stored""".split()
        S = {n: sem("s_" + n) for n in NAMES}
        S.update({(n, lane): sem(f"s_{n}_{lane}") for n in LANE_NAMES for lane in range(LANES)})
        DVE_STEPS = 5
        TAIL_STEPS = 7 * LANES

        START = {"mask_rows0": 16, "mask_rows1": 16, "den_full": 1, "norm_done": 2, "x1_ready": 1, "s_full": 1,
                 "p_ready": SBANKS, "av_done": PRING, "acc_done": PRING + 1}
        START.update({(n, lane): by for n, by in (("u_psum", 1), ("gate_ready", 1), ("out_stored", 16))
                      for lane in range(LANES)})

        def need(eng, name, b, per, k):
            eng.wait_ge(S[name], b * per + (k + START.get(name, 0)))

        def need_item(eng, name, b, ahead, item, back=0):
            value, per = count(name, ahead, item)
            twice = 2 if name == "k_hi" else 1
            need(eng, name, b, twice * per, twice * value - back)

        def emptied(eng, b, ahead, item):
            kind = EMPTIED_BY.get(item[0], item[0])
            need_item(eng, "dve_aux" if kind in COUNTED["dve_aux"] else "act_aux", b, ahead, (kind,) + item[1:])

        def split_mm(dst, parts):
            for n, (a, m) in enumerate(parts):
                mm = nc.tensor.matmul(dst, a, m, start=(n == 0), stop=(n == len(parts) - 1))
            return mm

        def rows_of(t):
            return P if t < KT - 1 else TAIL

        def turned(u):
            return u * TURN * P, min((u + 1) * TURN * P, KEYS)

        block = ctx.enter_context(nc.Block())

        @block.sync
        def _(sp):
            for name, value in START.items():
                sp.sem_inc(S[name], value)
            sp.dma_start(raw_kv, Wkv).then_inc(S["kv_in"], 16)
            for dst, src in (
                (wo[:, :, :], Wo.rearrange("(t p) n -> p t n", p=P)),
                (wq[:, :, :], Wq.rearrange("(t p) n -> p t n", p=P)),
                (raw_wg, W_gate.rearrange("(t p) n -> p t n", p=P)),
                (wm[:, :, :], W_mem.rearrange("(t p) n -> p t n", p=P)),
                (normrows[0:2, :], ln_q_g.rearrange("(t p) -> t p", p=P)),
                (normrows[2:4, :], ln_q_b.rearrange("(t p) -> t p", p=P)),
                (normrows[4:6, :], ln_ff_g.rearrange("(t p) -> t p", p=P)),
                (normrows[6:8, :], ln_ff_b.rearrange("(t p) -> t p", p=P)),
                (bgate[:, :], b_gate.rearrange("(a n) -> a n", a=1)),
                (gates[:, 0:1], attn_gate.rearrange("(a n) -> a n", a=1).broadcast_to([P, 1])),
                (gates[:, 1:2], ff_gate.rearrange("(a n) -> a n", a=1).broadcast_to([P, 1])),
            ):
                sp.dma_start(dst, src).then_inc(S["weights_in"], 16)
            sp.wait_ge(S["consts"], 1)
            for i in range(BATCH):
                sp.dma_start(xs[:, i, :, :], x_v[i, :, :, :]).then_inc(S["x_in"], 16)
            sp.dma_start(mask8[MASK_ROW:MASK_ROW + 1, :], media_mask[0:1, :]).then_inc(S["mask_in"], 16)
            sp.dma_start(nat0[:, 0:KT - 1, :], media_full[0, :, :, :]).then_inc(S["media_in"], 16)
            sp.dma_start(nat0[0:TAIL, KT - 1, :], media_tail[0, :, :]).then_inc(S["media_in"], 16)

            def copy_mask_row(slot, h):
                sp.dma_start(kk[MASK_ROW:MASK_ROW + 1, 1, slot, h, 0:KEYS].bitcast(F32),
                             kk[MASK_ROW:MASK_ROW + 1, 1, 0, 0, 0:KEYS].bitcast(F32))\
                    .then_inc(S[f"mask_rows{slot}"], 16)

            sp.wait_ge(S["mask_row_ready"], 1)
            for slot, h in ((0, 1), (1, 0), (1, 1)):
                copy_mask_row(slot, h)
            with sp.Fori(0, BATCH - 1) as b:
                sp.dma_start(mask8[MASK_ROW:MASK_ROW + 1, :], media_mask[bass.ds(b + 1, 1), :])\
                    .then_inc(S["mask_in"], 16)
                need(sp, "t_hi", b, TUNITS, TUNITS)
                sp.dma_start(nat0[:, 0:KT - 1, :], media_full[b + 1, :, :, :]).then_inc(S["media_in"], 16)
                sp.dma_start(nat0[0:TAIL, KT - 1, :], media_tail[b + 1, :, :]).then_inc(S["media_in"], 16)
                need(sp, "mask_row_ready", b, 1, 2)
                copy_mask_row(0, 1)
                need(sp, "s_full", b, NT, NT)
                for h in range(2):
                    copy_mask_row(1, h)
            sp.wait_ge(S["t_hi"], BATCH * TUNITS)
            need(sp, "s_full", BATCH, NT, 0)
            for dst, src in (
                (w1[:, :, :], W1.rearrange("(t p) n -> p t n", p=P)),
                (w2[:, :, :], W2.rearrange("(t p) n -> p t n", p=P)),
                (normw[:, :], norm_w.rearrange("(a n) -> a n", a=1).broadcast_to([P, DIM])),
            ):
                sp.dma_start(dst, src).then_inc(S["late_weights_in"], 16)
            with sp.Fori(0, BATCH // LANES) as it:
                for lane in range(LANES):
                    need(sp, ("u_psum", lane), it, 1, 0)
                    sp.dma_start(nats[lane][:, 0:KT - 1, :], media_full[it * LANES + lane, :, :, :])\
                        .then_inc(S["media_in", lane], 16)
                    sp.dma_start(nats[lane][0:TAIL, KT - 1, :], media_tail[it * LANES + lane, :, :])\
                        .then_inc(S["media_in", lane], 16)
                for lane in range(LANES):
                    need(sp, ("out_ready", lane), it, QT, QT)
                    sp.dma_start(out_v[it * LANES + lane, :, :, :], ress[lane][:, :, :]).then_inc(S["out_stored", lane], 16)
            for lane in range(LANES):
                sp.wait_ge(S["out_stored", lane], 16 * (BATCH // LANES) + START["out_stored", lane])

        @block.gpsimd
        def _(pool):
            nc.gpsimd.memset(ident[:, :], 0.0).then_inc(S["identity"], 1)
            pool.wait_ge(S["identity"], 1)
            nc.gpsimd.affine_select(out=ident[:, :], in_=ident[:, :], compare_op=ALU.not_equal, fill=1.0,
                                    base=0, pattern=[[-1, P]], channel_multiplier=1).then_inc(S["identity"], 1)
            nc.gpsimd.memset(mhalf[:, :], -0.5).then_inc(S["identity"], 1)
            pool.wait_ge(S["identity"], 3)

            def reciprocal_root(lane, done):
                nc.gpsimd.tensor_tensor(rstd[:, lane, :], var[:, lane, :], mhalf[:, :], ALU.pow).then_inc(S[done], 1)

            def sums(b, next_batch):
                for j in range(PAIRS):
                    n0 = j * GROUPS
                    need(pool, "p_ready", b, NT, j * KT + 4)
                    need(pool, "den_full", b, PAIRS, j)
                    nc.gpsimd.tensor_tensor(acc[:, :], pe_ring[:, n0 % PRING, :], pe_ring[:, (n0 + 1) % PRING, :],
                                            ALU.add).then_inc(S["acc_done"], 1)
                    if next_batch and j == PAIRS - 2:
                        need(pool, "var_ready", b, 1, 2)
                        reciprocal_root(0, "rstd_ready")
                    for g in range(2, GROUPS - 1):
                        need(pool, "p_ready", b, NT, j * KT + 2 * g + 2)
                        need(pool, "acc_done", b, NG, n0 + g - 1)
                        nc.gpsimd.tensor_tensor(acc[:, :], acc[:, :], pe_ring[:, (n0 + g) % PRING, :],
                                                ALU.add).then_inc(S["acc_done"], 1)
                    need(pool, "acc_done", b, NG, n0 + GROUPS - 2)
                    nc.gpsimd.tensor_tensor(acc[:, 0:512], acc[:, 0:512], acc[:, 512:1024],
                                            ALU.add).then_inc(S["acc_done"], 1)
                    need(pool, "p_ready", b, NT, (j + 1) * KT)
                    need(pool, "acc_done", b, NG, n0 + GROUPS - 1)
                    nc.gpsimd.tensor_tensor(acc[0:TAIL, 0:512], acc[0:TAIL, 0:512],
                                            pe_ring[0:TAIL, (n0 + GROUPS - 1) % PRING, 0:512],
                                            ALU.add).then_inc(S["acc_done"], 1)

            pool.wait_ge(S["var_ready"], 1)
            reciprocal_root(0, "rstd_ready")
            with pool.Fori(0, BATCH - 1) as b:
                sums(b, True)
            sums(BATCH - 1, False)
            with pool.Fori(0, BATCH // LANES) as it:
                for lane in range(LANES):
                    need(pool, ("var_ready", lane), it, 1, 1)
                    reciprocal_root(lane, ("rstd_ready", lane))
                for lane in range(LANES):
                    need(pool, ("ssq_ready", lane), it, 1, 1)
                    reciprocal_root(lane, ("rms_ready", lane))

        @block.scalar
        def _(act):
            act.wait_ge(S["kv_in"], 16)
            nc.scalar.copy(wk_hi[:, :], raw_kv[:, 0:INNER]).then_inc(S["kv_hi"], 1)
            nc.scalar.copy(wv_hi[:, :], raw_kv[:, INNER:2 * INNER]).then_inc(S["kv_hi"], 1)
            act.wait_ge(S["weights_in"], 16 * 11)
            nc.scalar.activation(gates[:, :], gates[:, :], ACT.Tanh).then_inc(S["gates_ready"], 1)
            act.wait_ge(S["wmt_psum"], 1)
            nc.scalar.copy(wmt[:, :], side[0][:, 0:DIM])
            nc.scalar.copy(wg[:, :, :], wide[:, 0:2 * DT * DIM].rearrange("p (f n) -> p f n", f=2 * DT))
            nc.scalar.copy(norms[:, :, :], side[0][:, DIM:DIM + 4 * DT].rearrange("p (a t) -> p a t", a=4))\
                .then_inc(S["wmt_ready"], 1)
            def attention(b, order):
                for ahead, item in order:
                    kind, j = item[0], None if len(item) == 1 else item[1]
                    if kind in COUNTED["aux_full"] and kind not in "MC":
                        need_item(act, "aux_full", b, ahead, item)
                        bank = aux[aux_bank(ahead, item)]
                    if kind == "T":
                        c0, c1 = turned(j)
                        nc.scalar.copy(mt_hi[:, c0:c1], bank[:, 0:c1 - c0]).then_inc(S["t_hi"], 1)
                    elif kind == "W":
                        nc.scalar.activation(zt[:, j, :], bank[:, 0:TOK], ACT.Identity,
                                             scale=norms[:, 0, j:j + 1], bias=norms[:, 1, j:j + 1])\
                            .then_inc(S["act_aux"], 1)
                    elif kind == "G":
                        if j == 0:
                            need_item(act, "dve_aux", b, ahead, ("C",))
                        if order is not FIRST:
                            need_item(act, "q_lo", b, 0, ("P", 2 * j + 1, 1))
                        nc.scalar.activation(qf[:, 2 * j:2 * j + 2, :], bank.rearrange("p (a q) -> p a q", a=2),
                                             ACT.Copy, scale=qs[:, 0:1]).then_inc(S["act_aux"], 1)
                    elif kind == "K":
                        c = item[2]
                        c0, c1 = CHUNKS[c]
                        if c == 0 and order is not FIRST:
                            need(act, "s_full", b, NT, (ahead * PAIRS + j - 1) * KT)
                        for h in range(2):
                            src = bank[h * HD:(h + 1) * HD, 0:c1 - c0]
                            nc.scalar.copy(kk[0:HD, :, j % 2, h, c0:c1],
                                           src.unsqueeze(1).broadcast_to([HD, 2, c1 - c0])).then_inc(S["k_hi"], 1)
                    elif kind == "V":
                        u = item[2]
                        if u == 0 and order is not FIRST:
                            need(act, "av_done", b, NG, (ahead * PAIRS + 2 * j - 2) * GROUPS)
                        n = rows_of(2 * u)
                        w = 2 if 2 * u + 1 < KT else 1
                        nc.scalar.copy(v[0:n, j % 2, 2 * u:2 * u + w, :],
                                       bank[0:n, 0:w * 256].rearrange("p (t n) -> p t n", t=w))\
                            .then_inc(S["act_aux"], 1)
                    elif kind == "R":
                        nc.scalar.copy(ql[ONE_ROW:ONE_ROW + 1, j % 2, :], bank[ONE_ROW:ONE_ROW + 1, :])\
                            .then_inc(S["act_aux"], 1)
                    elif kind == "S":
                        t = item[2]
                        jj = ahead * PAIRS + j
                        m, n, r = jj * KT + t, jj * GROUPS + t // 2, rows_of(t)
                        need(act, "s_full", b, NT, m + 1)
                        if t % 2 == 0:
                            need(act, "av_done", b, NG, n - PRING + 1)
                            need(act, "acc_done", b, NG, acc_count(n - PRING))
                        nc.scalar.activation(pe_ring[0:r, n % PRING, (t % 2) * 512:(t % 2 + 1) * 512],
                                             score_bank[m % SBANKS][0:r, :], ACT.Exp).then_inc(S["p_ready"], 1)

            attention(-1, FIRST)
            with act.Fori(0, BATCH - 1) as b:
                attention(b, BODY)
            attention(BATCH - 1, LAST)

            need(act, "x1_ready", BATCH, 1, 0)
            with act.Fori(0, BATCH // LANES) as it:
                for lane in range(LANES):
                    for half, (c0, c1) in enumerate(((0, 1024), (1024, KEYS))):
                        need(act, ("media_t_psum", lane), it, 2, half + 1)
                        nc.scalar.copy(mts_hi[lane][:, c0:c1], lane_psum[lane][:, c0:c1])\
                            .then_inc(S["media_hi", lane], 1)
                for lane in range(LANES):
                    need(act, ("zt_psum", lane), it, 1, 1)
                    for t in range(DT):
                        last = nc.scalar.activation(zts[lane][:, t, :], lane_bank[lane][0][:, t * TOK:(t + 1) * TOK],
                                                    ACT.Identity, scale=norms[:, 2, t:t + 1], bias=norms[:, 3, t:t + 1])
                    last.then_inc(S["zt_ready", lane], 1)
                for lane in range(LANES):
                    for half in range(2):
                        need(act, ("ff1_psum", lane), it, 2, half + 1)
                        nc.scalar.activation(gts[lane][:, 4 * half:4 * half + 4, :],
                                             lane_psum[lane][:, half * 1024:(half + 1) * 1024]
                                             .rearrange("p (c q) -> p c q", c=4),
                                             ACT.Gelu).then_inc(S["gelu_ready", lane], 1)
                for lane in range(LANES):
                    need(act, ("x2t_psum", lane), it, 1, 1)
                    nc.scalar.copy(zts[lane][:, :, :], lane_bank[lane][2].rearrange("p (t q) -> p t q", t=DT))\
                        .then_inc(S["x2t_ready", lane], 1)
                for lane in range(LANES):
                    need(act, ("gm_psum", lane), it, 1, 1)
                    nc.scalar.activation(gms_hi[lane][:, :], lane_bank[lane][3][:, 0:TOK], ACT.Copy, scale=L1_SCALE)\
                        .then_inc(S["gm_hi_ready", lane], 1)
                for t in range(QT):
                    for lane in range(LANES):
                        need(act, ("l1_max", lane), it, QT, t + 1)
                        nc.scalar.activation(p1s[lane][:, t, 0:KEYS], lane_psum[lane][:, 0:KEYS], ACT.Exp,
                                             bias=l1max[lane][:, t:t + 1],
                                             accum_out=l1den[lane][:, t:t + 1]).then_inc(S["l1_exp", lane], 1)
                for lane in range(LANES):
                    for u in range(0, GROUPS, 2):
                        need(act, ("pt_psum", lane), it, GROUPS, u + 1)
                        r = rows_of(2 * u)
                        w = 2 if 2 * u + 1 < KT else 1
                        nc.scalar.copy(pts[lane][0:r, 2 * u:2 * u + w, :],
                                       lane_bank[lane][u % 4][0:r, 0:w * TOK].rearrange("p (t q) -> p t q", t=w))\
                            .then_inc(S["pt_act", lane], 1)
                for lane in range(LANES):
                    need(act, ("u_psum", lane), it, 1, 1)
                    nc.scalar.copy(uts[lane][:, :], lane_bank[lane][3][:, 0:TOK]).then_inc(S["u_ready", lane], 1)
                for lane in range(LANES):
                    need(act, ("ct_psum", lane), it, 1, 1)
                    nc.scalar.copy(cts[lane][:, :, :], lane_bank[lane][2].rearrange("p (t q) -> p t q", t=DT))\
                        .then_inc(S["ct_ready", lane], 1)
                for lane in range(LANES):
                    need(act, ("gate_psum", lane), it, 1, 1)
                    nc.scalar.activation(gate_s[lane][:, :, :], lane_bank[lane][3].rearrange("p (t d) -> p t d", t=QT),
                                         ACT.Tanh, scale=0.5).then_inc(S["gate_ready", lane], 1)
                for lane in range(LANES):
                    need(act, ("fused_ready", lane), it, 1, 1)
                    for t in range(QT):
                        last = nc.scalar.activation(squares[lane][:, t, :], fuseds[lane][:, t, :], ACT.Square,
                                                    accum_out=l1sum[lane][:, t:t + 1])
                    last.then_inc(S["square_ready", lane], 1)

        @block.vector
        def _(dve):
            steps = [0]

            nc.vector.memset(ones[:, :], 1.0)
            nc.vector.memset(kk[HD:P, 1, :, :, :].bitcast(F32), 0.0)
            nc.vector.memset(qm[HD:KX, :].bitcast(F32), 0.0)
            nc.vector.memset(ql[HD:KX, :, :].bitcast(F32), 0.0)
            nc.vector.memset(mt_hi[:, KEYS:KPAD].bitcast(F32), 0.0)
            nc.vector.memset(mt_lo[:, KEYS:KPAD].bitcast(F32), 0.0).then_inc(S["dve_step"], 1)
            dve.wait_ge(S["dve_step"], 1)
            nc.vector.memset(kk[MASK_ROW:MASK_ROW + 1, 1, :, :, KEYS:KPAD].bitcast(F32), -BIG)
            nc.vector.memset(kk[ONE_ROW:ONE_ROW + 1, 1, :, :, :].bitcast(F32), 1.0)
            nc.vector.memset(qm[MASK_ROW:MASK_ROW + 1, :].bitcast(F32), 1.0)
            nc.vector.memset(ql[MASK_ROW:MASK_ROW + 1, :, :].bitcast(F32), 1.0).then_inc(S["consts"], 1)
            dve.wait_ge(S["kv_hi"], 1)
            nc.vector.tensor_tensor(wk_lo[:, :], raw_kv[:, 0:INNER], wk_hi[:, :].bitcast(F32), ALU.subtract)\
                .then_inc(S["kv_split"], 1)
            dve.wait_ge(S["kv_hi"], 2)
            nc.vector.tensor_tensor(wv_lo[:, :], raw_kv[:, INNER:2 * INNER], wv_hi[:, :].bitcast(F32), ALU.subtract)\
                .then_inc(S["kv_split"], 1)
            dve.wait_ge(S["gates_ready"], 1)
            dve.wait_ge(S["wmt_ready"], 1)

            dve.wait_ge(S["x_in"], 16 * BATCH)
            def attention(b, order):
                steps[0] = 0

                def step(instruction):
                    steps[0] += 1
                    instruction.then_inc(S["dve_step"], 1)
                    dve.wait_ge(S["dve_step"], b * DVE_STEPS + (DVE_STEPS + steps[0] + 1))

                for ahead, item in order:
                    kind, j = item[0], None if len(item) == 1 else item[1]
                    if kind == "X":
                        for t in range(QT):
                            last = nc.vector.bn_stats(stat[:, 0, t, :], xs[:, b + 1, t, :])
                        step(last)
                        nc.vector.memset(var[:, 0, :], 0.0)
                        for t in range(QT):
                            last = nc.vector.bn_aggr(mv[:, 0, t, :], stat[:, 0, t, :])
                        step(last)
                        nc.vector.tensor_scalar(var[:, 0, :], mv[:, 0, :, 1], LN_EPS, None, ALU.add)\
                            .then_inc(S["var_ready"], 1)
                    elif kind == "Z":
                        need(dve, "rstd_ready", b, 1, 2)
                        for t in range(QT):
                            last = nc.vector.tensor_scalar(z[:, t, :], xs[:, b + 1, t, :], mv[:, 0, t, 0:1],
                                                           rstd[:, 0, t:t + 1], ALU.subtract, ALU.mult)
                        last.then_inc(S["z_ready"], 1)
                    elif kind == "B":
                        r = slice(MASK_ROW, MASK_ROW + 1)
                        need(dve, "mask_in", b, 16, 32)
                        step(nc.vector.reduce_sum(msum[r, 0:1], mask8[r, :], axis=AX.X))
                        step(nc.vector.tensor_scalar(msum[r, 1:2], msum[r, 0:1], 0.5, None, ALU.is_le))
                        nc.vector.tensor_scalar(msum[r, 2:3], msum[r, 1:2], -Q_SCALE, Q_SCALE, ALU.mult, ALU.add)\
                            .then_inc(S["q_scale_ready"], 1)
                        step(nc.vector.tensor_scalar(msum[r, 3:4], msum[r, 1:2], -BIG, BIG, ALU.mult, ALU.add))
                    elif kind == "I":
                        r = slice(MASK_ROW, MASK_ROW + 1)
                        if order is not FIRST:
                            need(dve, "s_full", b, NT, (PAIRS - 1) * KT)
                            need(dve, "mask_rows1", b, 32, 32)
                        nc.vector.tensor_scalar(kk[r, 1, 0, 0, 0:KEYS], mask8[r, :], -1.0, msum[r, 3:4],
                                                ALU.add, ALU.mult).then_inc(S["mask_row_ready"], 1)
                    elif kind == "C":
                        need_item(dve, "aux_full", b, ahead, item)
                        nc.vector.tensor_copy(qs[:, :], aux[aux_bank(ahead, item)][:, 0:1]).then_inc(S["dve_aux"], 1)
                    elif kind == "U":
                        c0, c1 = turned(j)
                        need_item(dve, "t_hi", b, ahead, ("T", j))
                        nc.vector.tensor_tensor(mt_lo[:, c0:c1], aux[aux_bank(ahead, ("T", j))][:, 0:c1 - c0],
                                                mt_hi[:, c0:c1].bitcast(F32), ALU.subtract).then_inc(S["dve_aux"], 1)
                    elif kind == "Q":
                        h, s = item[2], j % 2
                        if h == 0:
                            need_item(dve, "act_aux", b, ahead, ("G", j // 2))
                            if order is not FIRST:
                                need(dve, "s_full", b, NT, (ahead * PAIRS + j - 1) * KT)
                            if order is not FIRST or j:
                                before = (ahead, j - 1) if j else (0, PAIRS - 1)
                                need_item(dve, "dve_aux", b, before[0], ("M", before[1], 1, 1, NCH - 1))
                        src = qf[h * HD:(h + 1) * HD, j, :]
                        cols = slice(h * TOK, (h + 1) * TOK)
                        nc.vector.tensor_copy(qh[0:HD, s, cols], src)
                        nc.vector.tensor_copy(qh[HD:P, s, cols], src)
                        nc.vector.tensor_copy(qm[0:HD, cols], src).then_inc(S["q_hi"], 1)
                    elif kind == "P":
                        h, s = item[2], j % 2
                        need_item(dve, "q_hi", b, ahead, ("Q", j, h))
                        part = slice(h * HD, (h + 1) * HD)
                        cols = slice(h * TOK, (h + 1) * TOK)
                        nc.vector.tensor_tensor(ql[0:HD, s, cols], qf[part, j, :], qh[part, s, cols].bitcast(F32),
                                                ALU.subtract).then_inc(S["q_lo"], 1)
                    elif kind == "L":
                        c0, c1 = CHUNKS[item[2]]
                        keys = ("K",) + item[1:]
                        bank, s = aux[aux_bank(ahead, keys)], j % 2
                        for h in range(2):
                            need_item(dve, "k_hi", b, ahead, keys, 1 - h)
                            last = nc.vector.tensor_tensor(kk[HD:P, 0, s, h, c0:c1], bank[h * HD:(h + 1) * HD, 0:c1 - c0],
                                                           kk[0:HD, 0, s, h, c0:c1].bitcast(F32), ALU.subtract)
                        last.then_inc(S["dve_aux"], 1)
                    elif kind == "M":
                        h, t, c = item[2:]
                        c0, c1 = CHUNKS[c]
                        need_item(dve, "aux_full", b, ahead, item)
                        nc.vector.reduce_max(mx[:, 2 * h + t, c:c + 1], aux[aux_bank(ahead, item)][:, 0:c1 - c0],
                                             axis=AX.X).then_inc(S["dve_aux"], 1)
                    elif kind == "N":
                        need_item(dve, "dve_aux", b, ahead, ("M", j, 1, 1, NCH - 1))
                        nc.vector.tensor_reduce(m4[:, :], mx[:, :, :], axis=AX.X, op=ALU.max).then_inc(S["m4_ready"], 1)
                        need_item(dve, "m4_ready", b, ahead, item)
                        nc.vector.tensor_scalar(negm[:, :], m4[:, :], -1.0, None, ALU.mult).then_inc(S["negm_ready"], 1)
                    elif kind == "E":
                        i, w = item[2], TOK // RECIPROCAL_PARTS
                        if i == 0:
                            need(dve, "norm_done", b, PAIRS, j)
                            need(dve, "den_full", b, PAIRS, j + 1)
                        nc.vector.reciprocal(rec[:, i * w:(i + 1) * w], o_bank[j % 2][:, TOK + i * w:TOK + (i + 1) * w])\
                            .then_inc(S["rec_ready"], 1)
                    elif kind == "F":
                        need(dve, "rec_ready", b, PAIRS * RECIPROCAL_PARTS, (j + 1) * RECIPROCAL_PARTS)
                        nc.vector.tensor_tensor(ot[:, j, :], o_bank[j % 2][:, 0:TOK], rec[:, :], ALU.mult)\
                            .then_inc(S["norm_done"], 1)
                    elif kind == "H":
                        need(dve, "attn_proj", b, 1, 1)
                        for t in range(QT):
                            last = nc.vector.scalar_tensor_tensor(
                                xs[:, b, t, :], o_bank[1][:, t * DIM:(t + 1) * DIM], gates[:, 0:1],
                                xs[:, b, t, :], ALU.mult, ALU.add)
                        last.then_inc(S["x1_ready"], 1)
                assert steps[0] in (0, DVE_STEPS), steps[0]

            dve.wait_ge(S["x_in"], 16 * BATCH)
            attention(-1, FIRST)
            with dve.Fori(0, BATCH - 1) as b:
                attention(b, BODY)
            attention(BATCH - 1, LAST)

            need(dve, "x1_ready", BATCH, 1, 0)
            for lane in range(LANES):
                nc.vector.memset(mts_hi[lane][:, KEYS:KPAD].bitcast(F32), 0.0)
                nc.vector.memset(mts_lo[lane][:, KEYS:KPAD].bitcast(F32), 0.0).then_inc(S["pad_ready", lane], 1)
            with dve.Fori(0, BATCH // LANES) as it:
                steps[0] = 0

                def step(instruction):
                    steps[0] += 1
                    instruction.then_inc(S["tail_step"], 1)
                    dve.wait_ge(S["tail_step"], it * TAIL_STEPS + steps[0])

                for lane in range(LANES):
                    for t in range(QT):
                        last = nc.vector.bn_stats(stat[:, lane, t, :], xs[:, it * LANES + lane, t, :])
                    step(last)
                    nc.vector.memset(var[:, lane, :], 0.0)
                    for t in range(QT):
                        last = nc.vector.bn_aggr(mv[:, lane, t, :], stat[:, lane, t, :])
                    step(last)
                    nc.vector.tensor_scalar(var[:, lane, :], mv[:, lane, :, 1], LN_EPS, None, ALU.add)\
                        .then_inc(S["var_ready", lane], 1)
                for lane in range(LANES):
                    need(dve, ("rstd_ready", lane), it, 1, 1)
                    for t in range(QT):
                        last = nc.vector.tensor_scalar(zs[lane][:, t, :], xs[:, it * LANES + lane, t, :],
                                                       mv[:, lane, t, 0:1], rstd[:, lane, t:t + 1],
                                                       ALU.subtract, ALU.mult)
                    last.then_inc(S["z_ready", lane], 1)
                for lane in range(LANES):
                    for half, (c0, c1) in enumerate(((0, 1024), (1024, KEYS))):
                        need(dve, ("media_hi", lane), it, 2, half + 1)
                        nc.vector.tensor_tensor(mts_lo[lane][:, c0:c1], lane_psum[lane][:, c0:c1],
                                                mts_hi[lane][:, c0:c1].bitcast(F32), ALU.subtract)\
                            .then_inc(S["media_lo", lane], 1)
                for lane in range(LANES):
                    for t in range(QT):
                        need(dve, ("ff2_psum", lane), it, QT, t + 1)
                        last = nc.vector.scalar_tensor_tensor(
                            x2s[lane][:, t, :], lane_bank[lane][t][:, 0:DIM], gates[:, 1:2],
                            xs[:, it * LANES + lane, t, :], ALU.mult, ALU.add)
                    last.then_inc(S["x2_ready", lane], 1)
                for lane in range(LANES):
                    need(dve, ("gm_hi_ready", lane), it, 1, 1)
                    nc.vector.scalar_tensor_tensor(gms_lo[lane][:, :], lane_bank[lane][3][:, 0:TOK], L1_SCALE,
                                                   gms_hi[lane][:, :].bitcast(F32), ALU.mult, ALU.subtract)\
                        .then_inc(S["gm_lo_ready", lane], 1)
                for t in range(QT):
                    for lane in range(LANES):
                        need(dve, ("l1_scores", lane), it, QT, t + 1)
                        step(nc.vector.reduce_max(l1top[lane][:, t:t + 1], lane_psum[lane][:, 0:KEYS], axis=AX.X))
                        nc.vector.tensor_scalar(l1max[lane][:, t:t + 1], l1top[lane][:, t:t + 1], -1.0, None, ALU.mult)\
                            .then_inc(S["l1_max", lane], 1)
                for lane in range(LANES):
                    for u in range(1, GROUPS, 2):
                        need(dve, ("pt_psum", lane), it, GROUPS, u + 1)
                        nc.vector.tensor_copy(pts[lane][:, 2 * u:2 * u + 2, :],
                                              lane_bank[lane][u % 4].rearrange("p (t q) -> p t q", t=2))\
                            .then_inc(S["pt_dve", lane], 1)
                for lane in range(LANES):
                    need(dve, ("l1_exp", lane), it, QT, QT)
                    step(nc.vector.reciprocal(l1rec[lane][:, :], l1den[lane][:, :]))
                    need(dve, ("ctx_psum", lane), it, 1, 1)
                    for t in range(QT):
                        last = nc.vector.tensor_scalar(cxs[lane][:, t, :], lane_bank[lane][1][:, t * DIM:(t + 1) * DIM],
                                                       l1rec[lane][:, t:t + 1], None, ALU.mult)
                    last.then_inc(S["ctx_ready", lane], 1)
                for lane in range(LANES):
                    gate, fused = gate_s[lane][:, :, :], fuseds[lane][:, :, :]
                    need(dve, ("gate_ready", lane), it, 1, 1)
                    step(nc.vector.tensor_scalar(gate, gate, 0.5, 0.5, ALU.mult, ALU.add))
                    step(nc.vector.tensor_tensor(fused, gate, cxs[lane][:, :, :], ALU.mult))
                    nc.vector.tensor_tensor(fused, fused, x2s[lane][:, :, :], ALU.add).then_inc(S["fused_ready", lane], 1)
                for lane in range(LANES):
                    need(dve, ("square_ready", lane), it, 1, 1)
                    nc.vector.tensor_scalar(var[:, lane, :], l1sum[lane][:, :], 1.0 / DIM, RMS_EPS, ALU.mult, ALU.add)\
                        .then_inc(S["ssq_ready", lane], 1)
                for lane in range(LANES):
                    need(dve, ("rms_ready", lane), it, 1, 1)
                    if lane == 0:
                        dve.wait_ge(S["late_weights_in"], 16 * 3)
                    need(dve, ("out_stored", lane), it, 16, 0)
                    for t in range(QT):
                        nc.vector.scalar_tensor_tensor(ress[lane][:, t, :], fuseds[lane][:, t, :],
                                                       rstd[:, lane, t:t + 1], normw[:, :],
                                                       ALU.mult, ALU.mult).then_inc(S["out_ready", lane], 1)
            assert steps[0] == TAIL_STEPS, steps[0]

        @block.tensor
        def _(pe):
            mm = nc.tensor.matmul
            pe.wait_ge(S["identity"], 3)
            pe.wait_ge(S["consts"], 1)
            pe.wait_ge(S["weights_in"], 16 * 11)
            for t in range(DT):
                last = nc.tensor.transpose(side[0][:, t * P:(t + 1) * P], wm[:, t, :], ident[:, :])
            for f in range(2 * DT):
                for t in range(DT):
                    nc.tensor.transpose(wide[:, f * DIM + t * P:f * DIM + (t + 1) * P],
                                        raw_wg[:, t, f * P:(f + 1) * P], ident[:, :])
            last = nc.tensor.transpose(side[0][:, DIM:DIM + 4 * DT], normrows[:, :], ident[0:4 * DT, 0:4 * DT])
            last.then_inc(S["wmt_psum"], 1)
            pe.wait_ge(S["wmt_ready"], 1)
            pe.wait_ge(S["kv_split"], 2)

            def transpose_tokens(dst, src):
                for t in range(DT):
                    for q in range(QT):
                        last = nc.tensor.transpose(dst[:, t * TOK + q * P:t * TOK + (q + 1) * P],
                                                   src[:, q, t * P:(t + 1) * P], ident[:, :])
                return last

            def attention(b, order):
                for ahead, item in order:
                    kind, j = item[0], None if len(item) == 1 else item[1]
                    if kind in COUNTED["aux_full"]:
                        bank = aux[aux_bank(ahead, item)]
                        if (order is FIRST, (ahead, item)) in AUX_BEFORE:
                            emptied(pe, b, *AUX_BEFORE[order is FIRST, (ahead, item)])
                    if kind == "T":
                        if j == 0:
                            need(pe, "media_in", b, 32, 64)
                        for i, t in enumerate(range(TURN * j, min(TURN * (j + 1), KT))):
                            r = rows_of(t)
                            last = nc.tensor.transpose(bank[:, i * P:i * P + r], nat0[0:r, t, :], ident[0:r, 0:r])
                        last.then_inc(S["aux_full"], 1)
                    elif kind == "W":
                        need(pe, "z_ready", b, 1, 2)
                        for q in range(QT):
                            last = nc.tensor.transpose(bank[:, q * P:(q + 1) * P], z[:, q, j * P:(j + 1) * P], ident[:, :])
                        last.then_inc(S["aux_full"], 1)
                    elif kind == "C":
                        need(pe, "q_scale_ready", b, 1, 2)
                        mm(bank[:, 0:1], ones[MASK_ROW:MASK_ROW + 1, :], msum[MASK_ROW:MASK_ROW + 1, 2:3],
                           start=True, stop=True).then_inc(S["aux_full"], 1)
                    elif kind == "G":
                        need_item(pe, "act_aux", b, ahead, ("W", DT - 1))
                        for i in range(2):
                            c0 = (2 * j + i) * P
                            for t in range(DT):
                                last = mm(bank[:, i * TOK:(i + 1) * TOK], wq[:, t, c0:c0 + P], zt[:, t, :],
                                          start=(t == 0), stop=(t == DT - 1))
                        last.then_inc(S["aux_full"], 1)
                    elif kind == "K":
                        if j == 0 and item[2] == 0:
                            need_item(pe, "dve_aux", b, ahead, ("U", TUNITS - 1))
                        c0, c1 = CHUNKS[item[2]]
                        w = slice(j * P, (j + 1) * P)
                        split_mm(bank[:, 0:c1 - c0], [(wk_hi[:, w], mt_hi[:, c0:c1]), (wk_hi[:, w], mt_lo[:, c0:c1]),
                                                      (wk_lo[:, w], mt_hi[:, c0:c1])]).then_inc(S["aux_full"], 1)
                    elif kind == "V":
                        w = slice(j * 256, (j + 1) * 256)
                        for i, t in enumerate(range(2 * item[2], min(2 * item[2] + 2, KT))):
                            r = rows_of(t)
                            k = slice(t * P, t * P + r)
                            last = split_mm(bank[0:r, i * 256:(i + 1) * 256],
                                            [(mt_hi[:, k], wv_hi[:, w]), (mt_hi[:, k], wv_lo[:, w]),
                                             (mt_lo[:, k], wv_hi[:, w])])
                        last.then_inc(S["aux_full"], 1)
                    elif kind == "M":
                        h, t, c = item[2:]
                        c0, c1 = CHUNKS[c]
                        if h == 0 and t == 0:
                            need_item(pe, "k_hi", b, ahead, ("K", j, c))
                            if c == 0:
                                need_item(pe, "q_hi", b, ahead, ("Q", j, 1))
                                if j < 2:
                                    need(pe, f"mask_rows{j}", b, 16 * (j + 1), 16 * (j + 1) * (1 + ahead))
                        q0 = h * TOK + t * P
                        mm(bank[:, 0:c1 - c0], qm[:, q0:q0 + P], kk[0:KX, 1, j % 2, h, c0:c1],
                           start=True, stop=True).then_inc(S["aux_full"], 1)
                    elif kind == "R":
                        need_item(pe, "negm_ready", b, ahead, ("N", j))
                        for i in range(4):
                            last = mm(bank[ONE_ROW:ONE_ROW + 1, i * P:(i + 1) * P], negm[:, i:i + 1], ident[:, :],
                                      start=True, stop=True)
                        last.then_inc(S["aux_full"], 1)
                    elif kind == "S":
                        t, s = item[2], j % 2
                        m = (ahead * PAIRS + j) * KT + t
                        if t == 0:
                            need_item(pe, "dve_aux", b, ahead, ("L", j, NCH - 1))
                            need_item(pe, "act_aux", b, ahead, ("R", j))
                            need_item(pe, "q_lo", b, ahead, ("P", j, 1))
                        need(pe, "p_ready", b, NT, m - SBANKS + 1)
                        r = rows_of(t)
                        k = slice(t * P, t * P + r)
                        for h in range(2):
                            q = slice(h * TOK, (h + 1) * TOK)
                            dst = score_bank[m % SBANKS][0:r, q]
                            mm(dst, kk[:, 0, s, h, k], qh[:, s, q], start=True, stop=False)
                            last = mm(dst, kk[0:KX, 1, s, h, k], ql[:, s, q], start=False, stop=True)
                        last.then_inc(S["s_full"], 1)
                    elif kind == "A":
                        t, s = item[2], j % 2
                        g, i = divmod(t, 2)
                        jj = ahead * PAIRS + j
                        n = jj * GROUPS + g
                        need(pe, "p_ready", b, NT, jj * KT + t + 1)
                        if t == 0:
                            if j == 1:
                                need(pe, "x1_ready", b, 1, ahead)
                            else:
                                need(pe, "norm_done", b, PAIRS, jj - 1)
                            need_item(pe, "act_aux", b, ahead, ("V", j // 2, GROUPS - 1))
                        r = rows_of(t)
                        for h in range(2):
                            d0 = (j % 2) * P + h * HD
                            last = mm(o_bank[s][h * HD:(h + 1) * HD, 0:TOK], v[0:r, (j // 2) % 2, t, d0:d0 + HD],
                                      pe_ring[0:r, n % PRING, i * 512 + h * TOK:i * 512 + (h + 1) * TOK],
                                      start=(t == 0), stop=(t == KT - 1))
                        if i == 1 or t == KT - 1:
                            last.then_inc(S["av_done"], 1)
                    elif kind == "D":
                        need(pe, "acc_done", b, NG, (j + 1) * GROUPS)
                        for h in range(2):
                            last = mm(o_bank[j % 2][h * HD:(h + 1) * HD, TOK:2 * TOK], ones[:, 0:HD],
                                      acc[:, h * TOK:(h + 1) * TOK], start=True, stop=True)
                        last.then_inc(S["den_full"], 1)
                    elif kind == "O":
                        t, part = item[1:]
                        if t == 0 and part == 0:
                            need(pe, "norm_done", b, PAIRS, PAIRS)
                        for i in range(part * PAIRS // 2, (part + 1) * PAIRS // 2):
                            last = mm(o_bank[1][:, t * DIM:(t + 1) * DIM], ot[:, i, t * P:(t + 1) * P], wo[:, i, :],
                                      start=(i == 0), stop=(i == PAIRS - 1))
                        if t == QT - 1 and part == 1:
                            last.then_inc(S["attn_proj"], 1)

            attention(-1, FIRST)
            with pe.Fori(0, BATCH - 1) as b:
                attention(b, BODY)
            attention(BATCH - 1, LAST)
            need(pe, "x1_ready", BATCH, 1, 0)

            with pe.Fori(0, BATCH // LANES) as it:
                for lane in range(LANES):
                    need(pe, ("gate_ready", lane), it, 1, 0)
                    need(pe, ("media_in", lane), it, 32, 32)
                    for t in range(KT):
                        r = rows_of(t)
                        last = nc.tensor.transpose(lane_psum[lane][:, t * P:t * P + r], nats[lane][0:r, t, :],
                                                   ident[0:r, 0:r])
                        if t in (7, KT - 1):
                            last.then_inc(S["media_t_psum", lane], 1)
                for lane in range(LANES):
                    need(pe, ("z_ready", lane), it, 1, 1)
                    need(pe, ("media_lo", lane), it, 2, 2)
                    transpose_tokens(lane_bank[lane][0], zs[lane]).then_inc(S["zt_psum", lane], 1)
                pe.wait_ge(S["late_weights_in"], 16 * 3)
                for lane in range(LANES):
                    need(pe, ("zt_ready", lane), it, 1, 1)
                    for f in range(FT):
                        for t in range(DT):
                            last = mm(lane_psum[lane][:, f * TOK:(f + 1) * TOK], w1[:, t, f * P:(f + 1) * P],
                                      zts[lane][:, t, :], start=(t == 0), stop=(t == DT - 1))
                        if f % 4 == 3:
                            last.then_inc(S["ff1_psum", lane], 1)
                for lane in range(LANES):
                    for t in range(QT):
                        for f in range(FT):
                            if t == 0 and f % 4 == 0:
                                need(pe, ("gelu_ready", lane), it, 2, f // 4 + 1)
                            last = mm(lane_bank[lane][t][:, 0:DIM], gts[lane][:, f, t * P:(t + 1) * P],
                                      w2[:, f, :], start=(f == 0), stop=(f == FT - 1))
                        last.then_inc(S["ff2_psum", lane], 1)
                for lane in range(LANES):
                    need(pe, ("x2_ready", lane), it, 1, 1)
                    transpose_tokens(lane_bank[lane][2], x2s[lane]).then_inc(S["x2t_psum", lane], 1)
                for lane in range(LANES):
                    need(pe, ("x2t_ready", lane), it, 1, 1)
                    for t in range(DT):
                        last = mm(lane_bank[lane][3][:, 0:TOK], wm[:, t, :], zts[lane][:, t, :],
                                  start=(t == 0), stop=(t == DT - 1))
                    last.then_inc(S["gm_psum", lane], 1)
                for t in range(QT):
                    for lane in range(LANES):
                        need(pe, *((("l1_exp", lane), it, QT, t) if t else (("gm_lo_ready", lane), it, 1, 1)))
                        q = slice(t * P, (t + 1) * P)
                        hi, lo = mts_hi[lane], mts_lo[lane]
                        for c0 in range(0, KPAD, 512):
                            c1 = min(c0 + 512, KPAD)
                            last = split_mm(lane_psum[lane][:, c0:c1], [(gms_hi[lane][:, q], hi[:, c0:c1]),
                                                                        (gms_hi[lane][:, q], lo[:, c0:c1]),
                                                                        (gms_lo[lane][:, q], hi[:, c0:c1])])
                        last.then_inc(S["l1_scores", lane], 1)
                for lane in range(LANES):
                    need(pe, ("l1_exp", lane), it, QT, QT)
                    for u in range(GROUPS):
                        if u >= 4:
                            w = u - 4
                            need(pe, *((("pt_dve", lane), it, GROUPS // 2) if w % 2 else
                                       (("pt_act", lane), it, GROUPS // 2 + 1)), w // 2 + 1)
                        for i, t in enumerate(range(2 * u, min(2 * u + 2, KT))):
                            r = rows_of(t)
                            for q in range(QT):
                                c0 = i * TOK + q * P
                                last = nc.tensor.transpose(lane_bank[lane][u % 4][0:r, c0:c0 + P],
                                                           p1s[lane][:, q, t * P:t * P + r], ident[:, :])
                        last.then_inc(S["pt_psum", lane], 1)
                for lane in range(LANES):
                    need(pe, ("pt_act", lane), it, GROUPS // 2 + 1, GROUPS // 2 + 1)
                    need(pe, ("pt_dve", lane), it, GROUPS // 2, GROUPS // 2)
                    for t in range(KT):
                        r = rows_of(t)
                        last = mm(lane_bank[lane][3][:, 0:TOK], nats[lane][0:r, t, :], pts[lane][0:r, t, :],
                                  start=(t == 0), stop=(t == KT - 1))
                    last.then_inc(S["u_psum", lane], 1)
                for lane in range(LANES):
                    need(pe, ("u_ready", lane), it, 1, 1)
                    for q in range(QT):
                        last = mm(lane_bank[lane][1][:, q * DIM:(q + 1) * DIM], uts[lane][:, q * P:(q + 1) * P],
                                  wmt[:, :], start=True, stop=True)
                    last.then_inc(S["ctx_psum", lane], 1)
                for lane in range(LANES):
                    need(pe, ("ctx_ready", lane), it, 1, 1)
                    transpose_tokens(lane_bank[lane][2], cxs[lane]).then_inc(S["ct_psum", lane], 1)
                for lane in range(LANES):
                    need(pe, ("ct_ready", lane), it, 1, 1)
                    for q in range(QT):
                        dst = lane_bank[lane][3][:, q * DIM:(q + 1) * DIM]
                        for t in range(DT):
                            mm(dst, zts[lane][:, t, q * P:(q + 1) * P], wg[:, t, :], start=(t == 0), stop=False)
                        for t in range(DT):
                            mm(dst, cts[lane][:, t, q * P:(q + 1) * P], wg[:, DT + t, :], start=False, stop=False)
                        last = mm(dst, ones[0:1, :], bgate[:, :], start=False, stop=True)
                    last.then_inc(S["gate_psum", lane], 1)


_INS = ['x', 'ctx_1024', 'mask_BxS2_bk0', 'L0_xattn_ln_q_g', 'L0_xattn_ln_q_b', 'L0_xattn_Wq', 'L0_xattn_Wkv',
        'L0_xattn_Wo', 'L0_xattn_attn_gate', 'L0_xattn_ln_ff_g', 'L0_xattn_ln_ff_b', 'L0_xattn_W1', 'L0_xattn_W2',
        'L0_xattn_ff_gate', 'L1_xattn_W_mem', 'L1_xattn_W_gate', 'L1_xattn_b_gate', 'L1_xattn_norm_w']


def kernel(**inputs):
    import numpy as _np
    import concourse.bacc as _bacc
    from concourse import mybir as _mybir
    from concourse.bass_utils import run_bass_kernel_spmd as _run

    nc = _bacc.Bacc("TRN2", target_bir_lowering=False, num_devices=1)
    arrays, args = {}, []
    for name in _INS:
        a = _np.ascontiguousarray(inputs[name])
        arrays[f"in_{name}_dram"] = a
        args.append(nc.dram_tensor(f"in_{name}_dram", a.shape, _mybir.dt.from_np(a.dtype), kind="ExternalInput").ap())
    shape = inputs['x'].shape
    args.append(nc.dram_tensor("out_0_dram", shape, _mybir.dt.float32, kind="ExternalOutput").ap())
    cross_attention_kernel(nc, *args)
    r = _run(nc, [arrays], core_ids=[0])
    return r.results[0]["out_0_dram"]
```

```python
import concourse.bass as bass
from concourse import mybir
from contextlib import ExitStack

F32 = mybir.dt.float32
F32R = mybir.dt.float32r
U8 = mybir.dt.uint8
ACT = mybir.ActivationFunctionType
ALU = mybir.AluOpType
AX = mybir.AxisListType

P = 128
BIG = 2.0 ** 100
LAG = 3
SPLIT_AT = 2
RECIPROCAL_PARTS = 4

FIRST_TURN = """S0 Q0 A10 S1 K0 A11 Q1 A12 S2 V0 P0 D L0 S3 A0 M0.0.0 M0.1.0 S4 K1 E0 L1 S5 K2 A1 E1 A2 E2 A3 L2 M0.0.1
                E3 K3 F L3 A4 M1.0.0 A5 S6 V1 S7 M1.1.0 O0.0 S8 M0.1.1 M0.0.3 A6 P1 M0.0.2 M0.1.2 M0.1.3 S9 S10 M1.0.2
                V2 A7 M1.1.2 O0.1 M1.0.1 S11 M1.0.3 M1.1.1 M1.1.3 N A8 O1.0 V3 S12 A9 R O1.1 H""".split()
ODD_TURN = """S0 Q0 K0 A10 S1 P0 Q1 L0 K1 S2 M0.0.0 A11 S3 A12 L1 M0.1.0 K2 D M1.0.0 S4 S5 L2 A0 K3 A1 E0 V4 E1 L3 A2
              A3 M0.0.1 S6 M0.0.2 M0.1.1 M0.0.3 M0.1.3 S7 M0.1.2 S8 M1.1.0 A4 M1.0.1 A5 V5 M1.1.1 M1.0.3 M1.0.2 S9 A6
              M1.1.2 M1.1.3 E2 E3 S10 V6 S11 A7 A8 N R F S12 A9 P1""".split()
EVEN_TURN = """S0 Q0 Q1 K0 K1 S1 K2 L0 P0 A10 L1 L2 A11 A12 S2 M0.0.0 A0 D E0 E1 V0 S3 V1 V2 M0.1.0 M0.0.1 M1.0.0 S4 K3
               A1 P1 M0.0.2 L3 S5 S6 M0.1.1 M0.1.2 A2 S7 M1.0.1 M1.0.2 M0.0.3 A3 M1.1.1 M0.1.3 S8 S9 M1.1.2 M1.1.0 A4
               A5 E2 E3 M1.0.3 V3 A6 M1.1.3 A7 S10 S11 A8 F N R A9 S12""".split()
LAST_BUT_ONE_TURN = """S0 A10 X K0 S1 A11 Q0 Q1 K1 B L0 K2 A12 L1 A0 L2 S2 S3 M0.0.0 D M0.1.0 Y A1 K3 A2 M0.0.1 L3 S4 S5 A3
                       M0.0.3 M0.0.2 S6 M0.1.3 M1.0.0 M0.1.2 S7 S8 M1.0.2 M1.1.0 A4 S9 M0.1.1 M1.0.1 M1.1.1 S10 S11 P0 M1.0.3
                       A5 M1.1.2 M1.1.3 S12 N A6 E0 P1 E1 E2 E3 A7 A8 R F A9 Z""".split()
LAST_TURN = """S0 T0 U0 T1 T2 S1 W0 W1 U1 T3 U2 A10 A11 A12 S2 U3 T4 C U4 A0 G0 I K0 K1 Q0 D Q1 S3 L0 G1 L1 V0 M0.0.0
               M0.1.0 A1 M0.0.1 E0 S4 K2 M1.0.0 L2 S5 P0 A2 E1 A3 K3 L3 G2 M0.1.1 G3 M0.0.3 M0.0.2 V1 E2 S6 M1.1.0 S7
               M0.1.3 A4 E3 S8 V2 M1.0.1 M1.1.1 A5 M0.1.2 S9 M1.0.3 V3 M1.0.2 S10 M1.1.2 M1.1.3 A6 A7 S11 V4 N F V5 P1
               R V6 A8 S12 A9""".split()


def attention_order(pairs, tiles):
    turns = {0: FIRST_TURN, pairs - 2: LAST_BUT_ONE_TURN, pairs - 1: LAST_TURN}
    order = []
    for j in range(pairs):
        ahead_before, before = (0, j - 1) if j else (-1, pairs - 1)
        ahead_next, following = (0, j + 1) if j + 1 < pairs else (1, 0)
        for word in turns.get(j, ODD_TURN if j % 2 else EVEN_TURN):
            kind, numbers = word[0], tuple(int(n) for n in word[1:].split(".") if n)
            if kind in "XYZBCITUWG":
                order.append((1, (kind,) + numbers))
            elif kind in "OH":
                order.append((ahead_before, (kind,) + numbers))
            elif kind in "DEF" or kind == "A" and numbers[0] >= tiles - LAG:
                order.append((ahead_before, (kind, before) + numbers))
            elif kind in "SA":
                order.append((0, (kind, j) + numbers))
            elif kind == "V":
                n = j // 2 + 1 if ahead_next == 0 else 0
                order.append((ahead_next, (kind, n) + numbers))
            else:
                order.append((ahead_next, (kind, following) + numbers))
        if j == 0:
            head = len(order)
    return order[head:] + [(ahead + 1, item) for ahead, item in order[:head]]


def cross_attention_kernel(nc, x, media, media_mask, ln_q_g, ln_q_b, Wq, Wkv, Wo, attn_gate,
                           ln_ff_g, ln_ff_b, W1, W2, ff_gate, W_mem, W_gate, b_gate, norm_w, out):
    BATCH, TOK, DIM = x.shape
    KEYS, MED = media.shape[1:]
    INNER = Wq.shape[1]
    FF = W1.shape[1]
    HD = 64
    PAIRS = INNER // (2 * HD)
    QT = TOK // P
    DT = DIM // P
    FT = FF // P
    KT = -(-KEYS // P)
    TAIL = KEYS - (KT - 1) * P
    GROUPS = -(-KT // 2)
    KPAD = KEYS + KEYS % 2
    assert QT == 2 and DT == 2 and MED == P and TOK == 256 and KT % 2 == 1
    CHUNKS = [(0, 402), (402, 802), (802, 1202), (1202, KPAD)]
    NCH = len(CHUNKS)
    PRING = 4
    LN_EPS, RMS_EPS = 1e-5, 1e-6
    Q_SCALE = HD ** -0.5
    L1_SCALE = float(DIM) ** -0.5
    MASK_ROW, ONE_ROW, KX = 64, 96, 97

    TURN = 3
    TUNITS = -(-KT // TURN)
    NG, NT = PAIRS * GROUPS, PAIRS * KT
    SBANKS, ABANKS = 2, 4
    BODY = attention_order(PAIRS, KT)
    assert (PAIRS, KT, GROUPS, NCH, TUNITS) == (8, 13, 7, 4, 5)
    FIRST = [key for key in BODY if key[0] == 1]
    LAST = [key for key in BODY if key[0] == 0]

    COUNTED = {"aux_full": "KVMRTWGC", "act_aux": "VRWG", "dve_aux": "LMUC", "k_hi": "K", "t_hi": "T", "q_hi": "Q",
               "q_lo": "P", "m4_ready": "N", "negm_ready": "N", "q_scale_ready": "B", "z_ready": "Z",
               "var_ready": "X", "rstd_ready": "Y", "mask_row_ready": "I"}
    EMPTIED_BY = {"K": "L", "T": "U"}

    def counts(name, order):
        some = [x for x in order if x[1][0] in COUNTED[name]]
        return {x: n + 1 for n, x in enumerate(some)}

    IN_FIRST, IN_BODY = ({n: counts(n, order) for n in COUNTED} for order in (FIRST, BODY))

    def count(name, ahead, item):
        per, before = len(IN_BODY[name]), len(IN_FIRST[name])
        if ahead or (0, item) in IN_BODY[name]:
            return before + IN_BODY[name][(ahead, item)], per
        return before + IN_BODY[name][(1, item)] - per, per

    def aux_bank(ahead, item):
        return (count("aux_full", ahead, item)[0] - 1) % ABANKS

    AUX_BEFORE = {}
    for order in (FIRST, BODY):
        some = [key for key in ([(0, i) for _, i in FIRST] if order is BODY else []) + order
                if key[1][0] in COUNTED["aux_full"]]
        for n, key in enumerate(some):
            if n >= ABANKS and (order is FIRST or n >= len(IN_FIRST["aux_full"])):
                AUX_BEFORE[order is FIRST, key] = some[n - ABANKS]
    assert len(IN_BODY["aux_full"]) % ABANKS == 0, len(IN_BODY["aux_full"])
    assert all(IN_BODY[n][x] - len(IN_BODY[n]) + len(IN_FIRST[n]) == k
               for n in COUNTED for x, k in IN_FIRST[n].items())

    def acc_count(n):
        if n < 0:
            return acc_count(n + NG) - NG
        j, g = divmod(n, GROUPS)
        return j * GROUPS + (1 if g <= 1 else g if g < GROUPS - 1 else GROUPS)

    x_v = x.rearrange("b (t p) d -> b p t d", p=P)
    out_v = out.rearrange("b (t p) d -> b p t d", p=P)
    media_full = media[:, 0:(KT - 1) * P, :].rearrange("b (t p) e -> b p t e", p=P)
    media_tail = media[:, (KT - 1) * P:KEYS, :]

    LANES = 2
    assert BATCH % LANES == 0

    with ExitStack() as ctx:
        phase = ExitStack()

        def sb(name, shape, dt=F32):
            return ctx.enter_context(nc.sbuf_tensor(name, shape, dt))

        def ph(name, shape, dt=F32):
            return phase.enter_context(nc.sbuf_tensor(name, shape, dt))

        def sem(name):
            return ctx.enter_context(nc.semaphore(name))

        ident = sb("ident", [P, P])
        ones = sb("ones", [P, P])
        mhalf = sb("mhalf", [P, QT])
        norms = sb("norms", [P, 4, DT])
        gates = sb("gates", [P, 2])
        xs = sb("xs", [P, BATCH, QT, DIM])
        stat = sb("stat", [P, LANES, QT, 6])
        mv = sb("mv", [P, LANES, QT, 2])
        var = sb("var", [P, LANES, QT])
        rstd = sb("rstd", [P, LANES, QT])
        nat0 = sb("nat0", [P, KT, MED])

        kk = ph("kk", [P, 2, 2, 2, KPAD], F32R)
        wk_hi, wk_lo = ph("wk_hi", [P, INNER], F32R), ph("wk_lo", [P, INNER], F32R)
        wv_hi, wv_lo = ph("wv_hi", [P, INNER], F32R), ph("wv_lo", [P, INNER], F32R)
        wo = ph("wo", [P, PAIRS, DIM])
        wq = ph("wq", [P, DT, INNER])
        normrows = ph("normrows", [4 * DT, P])
        mt_hi, mt_lo = ph("mt_hi", [MED, KPAD], F32R), ph("mt_lo", [MED, KPAD], F32R)
        mask8 = ph("mask8", [P, KEYS], U8)
        msum = ph("msum", [P, 4])
        qs = ph("qs", [P, 1])
        z = ph("z", [P, QT, DIM])
        zt = ph("zt", [P, DT, TOK])
        qf = ph("qf", [P, PAIRS, TOK])
        ot = ph("ot", [P, PAIRS, TOK])
        qh = ph("qh", [P, 2, 2 * TOK], F32R)
        qm = ph("qm", [KX, 2 * TOK], F32R)
        ql = ph("ql", [KX, 2, 2 * TOK], F32R)
        v = ph("v", [P, 2, KT, 2 * P])
        pe_ring = ph("p_ring", [P, PRING, 1024])
        stage = pe_ring[:, :, :].rearrange("p a b -> p (a b)")
        raw_kv = stage[:, 0:2 * INNER]
        acc = ph("acc", [P, 1024])
        mx = ph("mx", [P, 4, NCH])
        m4 = ph("m4", [P, 4])
        negm = ph("negm", [P, 4])
        rec = ph("rec", [P, TOK])
        phase.close()

        w1 = ph("w1", [P, DT, FF])
        raw_wg = ph("raw_wg", [P, DT, 2 * DIM])
        wm = ph("wm", [P, DT, MED])
        bgate = ph("bgate", [1, DIM])
        wg = ph("wg", [P, 2 * DT, DIM])
        wmt = ph("wmt", [MED, DIM])
        w2 = ph("w2", [P, FT, DIM])
        normw = ph("normw", [P, DIM])
        nat1 = ph("nat1", [P, KT, MED])
        nats = [nat0, nat1]

        def lanes(name, shape, dt=F32):
            return [ph(f"{name}{lane}", shape, dt) for lane in range(LANES)]

        mts_hi, mts_lo = lanes("t_mt_hi", [MED, KPAD], F32R), lanes("t_mt_lo", [MED, KPAD], F32R)
        zs = lanes("t_z", [P, QT, DIM])
        zts = lanes("t_zt", [P, DT, TOK])
        gts = lanes("t_gelu", [P, FT, TOK])
        x2s = lanes("t_x2", [P, QT, DIM])
        gms_hi, gms_lo = lanes("t_gm_hi", [MED, TOK], F32R), lanes("t_gm_lo", [MED, TOK], F32R)
        p1s = lanes("t_p1", [P, QT, KPAD])
        pts = lanes("t_pt", [P, KT, TOK])
        uts = lanes("t_u", [MED, TOK])
        cxs = lanes("t_cx", [P, QT, DIM])
        cts = lanes("t_ct", [P, DT, TOK])
        gate_s = lanes("t_gate", [P, QT, DIM])
        fuseds = lanes("t_fused", [P, QT, DIM])
        squares = lanes("t_square", [P, QT, DIM])
        ress = lanes("t_res", [P, QT, DIM])
        l1top = lanes("t_top", [P, 2])
        l1max = lanes("t_max", [P, QT])
        l1den = lanes("t_den", [P, QT])
        l1rec = lanes("t_rec", [P, QT])
        l1sum = lanes("t_sum", [P, QT])
        ctx.enter_context(phase)

        psum = ctx.enter_context(nc.psum_tensor("psum", [P, 4096], F32))
        score_bank, aux, o_bank = ([psum[:, 512 * i:512 * (i + 1)] for i in some]
                                   for some in (range(0, SBANKS), range(SBANKS, 6), range(6, 8)))
        wide = psum[:, 0:2048]
        side = [psum[:, 512 * i:512 * (i + 1)] for i in (4, 5)]
        lane_psum = [psum[:, 2048 * lane:2048 * (lane + 1)] for lane in range(LANES)]
        lane_bank = [[lane_psum[lane][:, 512 * i:512 * (i + 1)] for i in range(4)] for lane in range(LANES)]

        NAMES = """norms_in norms_psum norms_ready kv_in wq_in weights_in consts identity slot1_rows kv_hi kv_split gates_ready
            gate_weights_in wmt_psum wmt_ready late_weights_in
            x0_in x_in media_in mask_in mask_rows0 mask_rows1 mask_row_ready q_scale_ready var_ready rstd_ready z_ready
            t_hi q_hi q_lo aux_full act_aux dve_aux k_hi m4_ready negm_ready s_full p_ready av_done acc_done
            den_full rec_ready norm_done attn_proj x1_ready dve_step tail_step""".split()
        LANE_NAMES = """media_in media_t_psum media_hi media_lo pad_ready var_ready rstd_ready z_ready zt_psum zt_ready
            ff1_psum gelu_ready ff2_psum x2_ready x2t_psum x2t_ready gm_psum gm_hi_ready gm_lo_ready l1_scores
            l1_max l1_exp pt_psum pt_act pt_dve u_psum u_ready ctx_psum ctx_ready ct_psum ct_ready gate_psum
            gate_ready fused_ready square_ready ssq_ready rms_ready out_ready out_stored""".split()
        S = {n: sem("s_" + n) for n in NAMES}
        S.update({(n, lane): sem(f"s_{n}_{lane}") for n in LANE_NAMES for lane in range(LANES)})
        DVE_STEPS = 5
        TAIL_STEPS = 7 * LANES

        START = {"mask_rows0": 16, "mask_rows1": 16, "den_full": 1, "norm_done": 2, "x1_ready": 1, "s_full": 1,
                 "p_ready": SBANKS, "av_done": PRING, "acc_done": PRING + 1}
        START.update({(n, lane): by for n, by in (("u_psum", 1), ("gate_ready", 1), ("out_stored", 16))
                      for lane in range(LANES)})

        def need(eng, name, b, per, k):
            eng.wait_ge(S[name], b * per + (k + START.get(name, 0)))

        def need_item(eng, name, b, ahead, item, back=0):
            value, per = count(name, ahead, item)
            twice = 2 if name == "k_hi" else 1
            need(eng, name, b, twice * per, twice * value - back)

        def emptied(eng, b, ahead, item):
            kind = EMPTIED_BY.get(item[0], item[0])
            need_item(eng, "dve_aux" if kind in COUNTED["dve_aux"] else "act_aux", b, ahead, (kind,) + item[1:])

        def split_mm(dst, parts):
            for n, (a, m) in enumerate(parts):
                mm = nc.tensor.matmul(dst, a, m, start=(n == 0), stop=(n == len(parts) - 1))
            return mm

        def rows_of(t):
            return P if t < KT - 1 else TAIL

        def turned(u):
            return u * TURN * P, min((u + 1) * TURN * P, KEYS)

        block = ctx.enter_context(nc.Block())

        @block.sync
        def _(sp):
            for name, value in START.items():
                sp.sem_inc(S[name], value)
            sp.dma_start(xs[:, 0, :, :], x_v[0, :, :, :]).then_inc(S["x0_in"], 16)
            sp.dma_start(nat0[:, 0:KT - 1, :], media_full[0, :, :, :]).then_inc(S["media_in"], 16)
            sp.dma_start(nat0[0:TAIL, KT - 1, :], media_tail[0, :, :]).then_inc(S["media_in"], 16)
            sp.dma_start(mask8[MASK_ROW:MASK_ROW + 1, :], media_mask[0:1, :]).then_inc(S["mask_in"], 16)
            for i, row in enumerate((ln_q_g, ln_q_b, ln_ff_g, ln_ff_b)):
                sp.dma_start(normrows[i * DT:(i + 1) * DT, :], row.rearrange("(t p) -> t p", p=P))\
                    .then_inc(S["norms_in"], 16)
            sp.dma_start(raw_kv, Wkv).then_inc(S["kv_in"], 16)
            sp.dma_start(wq[:, :, :], Wq.rearrange("(t p) n -> p t n", p=P)).then_inc(S["wq_in"], 16)
            for dst, src in (
                (wo[:, :, :], Wo.rearrange("(t p) n -> p t n", p=P)),
                (gates[:, 0:1], attn_gate.rearrange("(a n) -> a n", a=1).broadcast_to([P, 1])),
                (gates[:, 1:2], ff_gate.rearrange("(a n) -> a n", a=1).broadcast_to([P, 1])),
            ):
                sp.dma_start(dst, src).then_inc(S["weights_in"], 16)
            for i in range(1, BATCH):
                sp.dma_start(xs[:, i, :, :], x_v[i, :, :, :]).then_inc(S["x_in"], 16)

            def copy_mask_row(slot, h):
                sp.dma_start(kk[MASK_ROW:MASK_ROW + 1, 1, slot, h, 0:KEYS].bitcast(F32),
                             kk[MASK_ROW:MASK_ROW + 1, 1, 0, 0, 0:KEYS].bitcast(F32))\
                    .then_inc(S[f"mask_rows{slot}"], 16)

            sp.wait_ge(S["mask_row_ready"], 1)
            copy_mask_row(0, 1)
            sp.wait_ge(S["slot1_rows"], 3)
            for h in range(2):
                copy_mask_row(1, h)
            with sp.Fori(0, BATCH - 1) as b:
                sp.dma_start(mask8[MASK_ROW:MASK_ROW + 1, :], media_mask[bass.ds(b + 1, 1), :])\
                    .then_inc(S["mask_in"], 16)
                need(sp, "t_hi", b, TUNITS, TUNITS)
                sp.dma_start(nat0[:, 0:KT - 1, :], media_full[b + 1, :, :, :]).then_inc(S["media_in"], 16)
                sp.dma_start(nat0[0:TAIL, KT - 1, :], media_tail[b + 1, :, :]).then_inc(S["media_in"], 16)
                need(sp, "mask_row_ready", b, 1, 2)
                copy_mask_row(0, 1)
                need(sp, "s_full", b, NT, NT)
                for h in range(2):
                    copy_mask_row(1, h)
            sp.wait_ge(S["t_hi"], BATCH * TUNITS)
            need(sp, "s_full", BATCH, NT, 0)
            for dst, src in (
                (raw_wg[:, :, :], W_gate.rearrange("(t p) n -> p t n", p=P)),
                (wm[:, :, :], W_mem.rearrange("(t p) n -> p t n", p=P)),
                (bgate[:, :], b_gate.rearrange("(a n) -> a n", a=1)),
            ):
                sp.dma_start(dst, src).then_inc(S["gate_weights_in"], 16)
            for dst, src in (
                (w1[:, :, :], W1.rearrange("(t p) n -> p t n", p=P)),
                (w2[:, :, :], W2.rearrange("(t p) n -> p t n", p=P)),
                (normw[:, :], norm_w.rearrange("(a n) -> a n", a=1).broadcast_to([P, DIM])),
            ):
                sp.dma_start(dst, src).then_inc(S["late_weights_in"], 16)
            with sp.Fori(0, BATCH // LANES) as it:
                for lane in range(LANES):
                    need(sp, ("u_psum", lane), it, 1, 0)
                    sp.dma_start(nats[lane][:, 0:KT - 1, :], media_full[it * LANES + lane, :, :, :])\
                        .then_inc(S["media_in", lane], 16)
                    sp.dma_start(nats[lane][0:TAIL, KT - 1, :], media_tail[it * LANES + lane, :, :])\
                        .then_inc(S["media_in", lane], 16)
                for lane in range(LANES):
                    need(sp, ("out_ready", lane), it, QT, QT)
                    sp.dma_start(out_v[it * LANES + lane, :, :, :], ress[lane][:, :, :]).then_inc(S["out_stored", lane], 16)
            for lane in range(LANES):
                sp.wait_ge(S["out_stored", lane], 16 * (BATCH // LANES) + START["out_stored", lane])

        @block.gpsimd
        def _(pool):
            nc.gpsimd.memset(ident[:, :], 0.0).then_inc(S["identity"], 1)
            pool.wait_ge(S["identity"], 1)
            nc.gpsimd.affine_select(out=ident[:, :], in_=ident[:, :], compare_op=ALU.not_equal, fill=1.0,
                                    base=0, pattern=[[-1, P]], channel_multiplier=1).then_inc(S["identity"], 1)
            nc.gpsimd.memset(mhalf[:, :], -0.5).then_inc(S["identity"], 1)
            pool.wait_ge(S["identity"], 3)
            nc.gpsimd.memset(kk[ONE_ROW:ONE_ROW + 1, 1, 0, :, :].bitcast(F32), 1.0).then_inc(S["identity"], 1)

            def reciprocal_root(lane, done):
                nc.gpsimd.tensor_tensor(rstd[:, lane, :], var[:, lane, :], mhalf[:, :], ALU.pow).then_inc(S[done], 1)

            def sums(b, next_batch):
                for j in range(PAIRS):
                    n0 = j * GROUPS
                    need(pool, "p_ready", b, NT, j * KT + 4)
                    need(pool, "den_full", b, PAIRS, j)
                    nc.gpsimd.tensor_tensor(acc[:, :], pe_ring[:, n0 % PRING, :], pe_ring[:, (n0 + 1) % PRING, :],
                                            ALU.add).then_inc(S["acc_done"], 1)
                    if next_batch and j == PAIRS - 2:
                        need(pool, "var_ready", b, 1, 2)
                        reciprocal_root(0, "rstd_ready")
                    for g in range(2, GROUPS - 1):
                        need(pool, "p_ready", b, NT, j * KT + 2 * g + 2)
                        need(pool, "acc_done", b, NG, n0 + g - 1)
                        nc.gpsimd.tensor_tensor(acc[:, :], acc[:, :], pe_ring[:, (n0 + g) % PRING, :],
                                                ALU.add).then_inc(S["acc_done"], 1)
                    need(pool, "acc_done", b, NG, n0 + GROUPS - 2)
                    nc.gpsimd.tensor_tensor(acc[:, 0:512], acc[:, 0:512], acc[:, 512:1024],
                                            ALU.add).then_inc(S["acc_done"], 1)
                    need(pool, "p_ready", b, NT, (j + 1) * KT)
                    need(pool, "acc_done", b, NG, n0 + GROUPS - 1)
                    nc.gpsimd.tensor_tensor(acc[0:TAIL, 0:512], acc[0:TAIL, 0:512],
                                            pe_ring[0:TAIL, (n0 + GROUPS - 1) % PRING, 0:512],
                                            ALU.add).then_inc(S["acc_done"], 1)

            pool.wait_ge(S["identity"], 4)
            pool.wait_ge(S["var_ready"], 1)
            reciprocal_root(0, "rstd_ready")
            pool.wait_ge(S["rstd_ready"], 1)
            nc.gpsimd.memset(kk[HD:ONE_ROW, 1, 1, :, :].bitcast(F32), 0.0).then_inc(S["slot1_rows"], 1)
            pool.wait_ge(S["slot1_rows"], 1)
            nc.gpsimd.memset(kk[MASK_ROW:MASK_ROW + 1, 1, 1, :, KEYS:KPAD].bitcast(F32), -BIG)\
                .then_inc(S["slot1_rows"], 1)
            nc.gpsimd.memset(kk[ONE_ROW:ONE_ROW + 1, 1, 1, :, :].bitcast(F32), 1.0).then_inc(S["slot1_rows"], 1)
            pool.wait_ge(S["slot1_rows"], 3)
            with pool.Fori(0, BATCH - 1) as b:
                sums(b, True)
            sums(BATCH - 1, False)
            with pool.Fori(0, BATCH // LANES) as it:
                for lane in range(LANES):
                    need(pool, ("var_ready", lane), it, 1, 1)
                    reciprocal_root(lane, ("rstd_ready", lane))
                for lane in range(LANES):
                    need(pool, ("ssq_ready", lane), it, 1, 1)
                    reciprocal_root(lane, ("rms_ready", lane))

        @block.scalar
        def _(act):
            def attention(b, order):
                for ahead, item in order:
                    kind, j = item[0], None if len(item) == 1 else item[1]
                    if order is FIRST and item == ("W", 0):
                        act.wait_ge(S["norms_psum"], 1)
                        nc.scalar.copy(norms[:, :, :], o_bank[1][:, 0:4 * DT].rearrange("p (a t) -> p a t", a=4))\
                            .then_inc(S["norms_ready"], 1)
                        act.wait_ge(S["norms_ready"], 1)
                    if order is FIRST and item == ("T", SPLIT_AT):
                        act.wait_ge(S["kv_in"], 16)
                        nc.scalar.copy(wk_hi[:, :], raw_kv[:, 0:INNER]).then_inc(S["kv_hi"], 1)
                        nc.scalar.copy(wv_hi[:, :], raw_kv[:, INNER:2 * INNER]).then_inc(S["kv_hi"], 1)
                    if kind in COUNTED["aux_full"] and kind not in "MC":
                        need_item(act, "aux_full", b, ahead, item)
                        bank = aux[aux_bank(ahead, item)]
                    if kind == "T":
                        c0, c1 = turned(j)
                        nc.scalar.copy(mt_hi[:, c0:c1], bank[:, 0:c1 - c0]).then_inc(S["t_hi"], 1)
                    elif kind == "W":
                        nc.scalar.activation(zt[:, j, :], bank[:, 0:TOK], ACT.Identity,
                                             scale=norms[:, 0, j:j + 1], bias=norms[:, 1, j:j + 1])\
                            .then_inc(S["act_aux"], 1)
                    elif kind == "G":
                        if j == 0:
                            need_item(act, "dve_aux", b, ahead, ("C",))
                        if order is not FIRST:
                            need_item(act, "q_lo", b, 0, ("P", 2 * j + 1, 1))
                        nc.scalar.activation(qf[:, 2 * j:2 * j + 2, :], bank.rearrange("p (a q) -> p a q", a=2),
                                             ACT.Copy, scale=qs[:, 0:1]).then_inc(S["act_aux"], 1)
                    elif kind == "K":
                        c = item[2]
                        c0, c1 = CHUNKS[c]
                        if c == 0 and order is not FIRST:
                            need(act, "s_full", b, NT, (ahead * PAIRS + j - 1) * KT)
                        for h in range(2):
                            src = bank[h * HD:(h + 1) * HD, 0:c1 - c0]
                            nc.scalar.copy(kk[0:HD, :, j % 2, h, c0:c1],
                                           src.unsqueeze(1).broadcast_to([HD, 2, c1 - c0])).then_inc(S["k_hi"], 1)
                    elif kind == "V":
                        u = item[2]
                        if u == 0 and order is not FIRST:
                            need(act, "av_done", b, NG, (ahead * PAIRS + 2 * j - 2) * GROUPS)
                        n = rows_of(2 * u)
                        w = 2 if 2 * u + 1 < KT else 1
                        nc.scalar.copy(v[0:n, j % 2, 2 * u:2 * u + w, :],
                                       bank[0:n, 0:w * 256].rearrange("p (t n) -> p t n", t=w))\
                            .then_inc(S["act_aux"], 1)
                    elif kind == "R":
                        nc.scalar.copy(ql[ONE_ROW:ONE_ROW + 1, j % 2, :], bank[ONE_ROW:ONE_ROW + 1, :])\
                            .then_inc(S["act_aux"], 1)
                    elif kind == "S":
                        t = item[2]
                        jj = ahead * PAIRS + j
                        m, n, r = jj * KT + t, jj * GROUPS + t // 2, rows_of(t)
                        need(act, "s_full", b, NT, m + 1)
                        if t % 2 == 0:
                            need(act, "av_done", b, NG, n - PRING + 1)
                            need(act, "acc_done", b, NG, acc_count(n - PRING))
                        nc.scalar.activation(pe_ring[0:r, n % PRING, (t % 2) * 512:(t % 2 + 1) * 512],
                                             score_bank[m % SBANKS][0:r, :], ACT.Exp).then_inc(S["p_ready"], 1)

            attention(-1, FIRST)
            act.wait_ge(S["weights_in"], 16 * 3)
            nc.scalar.activation(gates[:, :], gates[:, :], ACT.Tanh).then_inc(S["gates_ready"], 1)
            with act.Fori(0, BATCH - 1) as b:
                attention(b, BODY)
            attention(BATCH - 1, LAST)

            act.wait_ge(S["wmt_psum"], 1)
            nc.scalar.copy(wg[:, :, :], wide[:, 0:2 * DT * DIM].rearrange("p (f n) -> p f n", f=2 * DT))
            nc.scalar.copy(wmt[:, :], side[0][:, 0:DIM]).then_inc(S["wmt_ready"], 1)
            need(act, "x1_ready", BATCH, 1, 0)
            with act.Fori(0, BATCH // LANES) as it:
                for lane in range(LANES):
                    for half, (c0, c1) in enumerate(((0, 1024), (1024, KEYS))):
                        need(act, ("media_t_psum", lane), it, 2, half + 1)
                        nc.scalar.copy(mts_hi[lane][:, c0:c1], lane_psum[lane][:, c0:c1])\
                            .then_inc(S["media_hi", lane], 1)
                for lane in range(LANES):
                    need(act, ("zt_psum", lane), it, 1, 1)
                    for t in range(DT):
                        last = nc.scalar.activation(zts[lane][:, t, :], lane_bank[lane][0][:, t * TOK:(t + 1) * TOK],
                                                    ACT.Identity, scale=norms[:, 2, t:t + 1], bias=norms[:, 3, t:t + 1])
                    last.then_inc(S["zt_ready", lane], 1)
                for lane in range(LANES):
                    for half in range(2):
                        need(act, ("ff1_psum", lane), it, 2, half + 1)
                        nc.scalar.activation(gts[lane][:, 4 * half:4 * half + 4, :],
                                             lane_psum[lane][:, half * 1024:(half + 1) * 1024]
                                             .rearrange("p (c q) -> p c q", c=4),
                                             ACT.Gelu).then_inc(S["gelu_ready", lane], 1)
                for lane in range(LANES):
                    need(act, ("x2t_psum", lane), it, 1, 1)
                    nc.scalar.copy(zts[lane][:, :, :], lane_bank[lane][2].rearrange("p (t q) -> p t q", t=DT))\
                        .then_inc(S["x2t_ready", lane], 1)
                for lane in range(LANES):
                    need(act, ("gm_psum", lane), it, 1, 1)
                    nc.scalar.activation(gms_hi[lane][:, :], lane_bank[lane][3][:, 0:TOK], ACT.Copy, scale=L1_SCALE)\
                        .then_inc(S["gm_hi_ready", lane], 1)
                for t in range(QT):
                    for lane in range(LANES):
                        need(act, ("l1_max", lane), it, QT, t + 1)
                        nc.scalar.activation(p1s[lane][:, t, 0:KEYS], lane_psum[lane][:, 0:KEYS], ACT.Exp,
                                             bias=l1max[lane][:, t:t + 1],
                                             accum_out=l1den[lane][:, t:t + 1]).then_inc(S["l1_exp", lane], 1)
                for lane in range(LANES):
                    for u in range(0, GROUPS, 2):
                        need(act, ("pt_psum", lane), it, GROUPS, u + 1)
                        r = rows_of(2 * u)
                        w = 2 if 2 * u + 1 < KT else 1
                        nc.scalar.copy(pts[lane][0:r, 2 * u:2 * u + w, :],
                                       lane_bank[lane][u % 4][0:r, 0:w * TOK].rearrange("p (t q) -> p t q", t=w))\
                            .then_inc(S["pt_act", lane], 1)
                for lane in range(LANES):
                    need(act, ("u_psum", lane), it, 1, 1)
                    nc.scalar.copy(uts[lane][:, :], lane_bank[lane][3][:, 0:TOK]).then_inc(S["u_ready", lane], 1)
                for lane in range(LANES):
                    need(act, ("ct_psum", lane), it, 1, 1)
                    nc.scalar.copy(cts[lane][:, :, :], lane_bank[lane][2].rearrange("p (t q) -> p t q", t=DT))\
                        .then_inc(S["ct_ready", lane], 1)
                for lane in range(LANES):
                    need(act, ("gate_psum", lane), it, 1, 1)
                    nc.scalar.activation(gate_s[lane][:, :, :], lane_bank[lane][3].rearrange("p (t d) -> p t d", t=QT),
                                         ACT.Tanh, scale=0.5).then_inc(S["gate_ready", lane], 1)
                for lane in range(LANES):
                    need(act, ("fused_ready", lane), it, 1, 1)
                    for t in range(QT):
                        last = nc.scalar.activation(squares[lane][:, t, :], fuseds[lane][:, t, :], ACT.Square,
                                                    accum_out=l1sum[lane][:, t:t + 1])
                    last.then_inc(S["square_ready", lane], 1)

        @block.vector
        def _(dve):
            steps = [0]

            nc.vector.memset(ones[:, :], 1.0)
            nc.vector.memset(kk[HD:ONE_ROW, 1, 0, :, :].bitcast(F32), 0.0)
            nc.vector.memset(qm[HD:KX, :].bitcast(F32), 0.0)
            nc.vector.memset(ql[HD:KX, :, :].bitcast(F32), 0.0)
            nc.vector.memset(mt_hi[:, KEYS:KPAD].bitcast(F32), 0.0)
            nc.vector.memset(mt_lo[:, KEYS:KPAD].bitcast(F32), 0.0).then_inc(S["dve_step"], 1)
            dve.wait_ge(S["dve_step"], 1)
            nc.vector.memset(kk[MASK_ROW:MASK_ROW + 1, 1, 0, :, KEYS:KPAD].bitcast(F32), -BIG)
            nc.vector.memset(qm[MASK_ROW:MASK_ROW + 1, :].bitcast(F32), 1.0)
            nc.vector.memset(ql[MASK_ROW:MASK_ROW + 1, :, :].bitcast(F32), 1.0).then_inc(S["consts"], 1)
            dve.wait_ge(S["x0_in"], 16)

            def attention(b, order):
                steps[0] = 0

                def step(instruction):
                    steps[0] += 1
                    instruction.then_inc(S["dve_step"], 1)
                    dve.wait_ge(S["dve_step"], b * DVE_STEPS + (DVE_STEPS + steps[0] + 1))

                for ahead, item in order:
                    kind, j = item[0], None if len(item) == 1 else item[1]
                    if order is FIRST and item == ("T", SPLIT_AT):
                        for i, (lo, hi) in enumerate(((wk_lo, wk_hi), (wv_lo, wv_hi))):
                            dve.wait_ge(S["kv_hi"], i + 1)
                            nc.vector.tensor_tensor(lo[:, :], raw_kv[:, i * INNER:(i + 1) * INNER],
                                                    hi[:, :].bitcast(F32), ALU.subtract).then_inc(S["kv_split"], 1)
                    if kind == "X":
                        for t in range(QT):
                            last = nc.vector.bn_stats(stat[:, 0, t, :], xs[:, b + 1, t, :])
                        step(last)
                        nc.vector.memset(var[:, 0, :], 0.0)
                        for t in range(QT):
                            last = nc.vector.bn_aggr(mv[:, 0, t, :], stat[:, 0, t, :])
                        step(last)
                        nc.vector.tensor_scalar(var[:, 0, :], mv[:, 0, :, 1], LN_EPS, None, ALU.add)\
                            .then_inc(S["var_ready"], 1)
                    elif kind == "Z":
                        need(dve, "rstd_ready", b, 1, 2)
                        for t in range(QT):
                            last = nc.vector.tensor_scalar(z[:, t, :], xs[:, b + 1, t, :], mv[:, 0, t, 0:1],
                                                           rstd[:, 0, t:t + 1], ALU.subtract, ALU.mult)
                        last.then_inc(S["z_ready"], 1)
                    elif kind == "B":
                        r = slice(MASK_ROW, MASK_ROW + 1)
                        need(dve, "mask_in", b, 16, 32)
                        step(nc.vector.reduce_sum(msum[r, 0:1], mask8[r, :], axis=AX.X))
                        step(nc.vector.tensor_scalar(msum[r, 1:2], msum[r, 0:1], 0.5, None, ALU.is_le))
                        nc.vector.tensor_scalar(msum[r, 2:3], msum[r, 1:2], -Q_SCALE, Q_SCALE, ALU.mult, ALU.add)\
                            .then_inc(S["q_scale_ready"], 1)
                        step(nc.vector.tensor_scalar(msum[r, 3:4], msum[r, 1:2], -BIG, BIG, ALU.mult, ALU.add))
                    elif kind == "I":
                        r = slice(MASK_ROW, MASK_ROW + 1)
                        if order is FIRST:
                            dve.wait_ge(S["consts"], 1)
                            dve.wait_ge(S["identity"], 4)
                        else:
                            need(dve, "s_full", b, NT, (PAIRS - 1) * KT)
                            need(dve, "mask_rows1", b, 32, 32)
                        nc.vector.tensor_scalar(kk[r, 1, 0, 0, 0:KEYS], mask8[r, :], -1.0, msum[r, 3:4],
                                                ALU.add, ALU.mult).then_inc(S["mask_row_ready"], 1)
                    elif kind == "C":
                        need_item(dve, "aux_full", b, ahead, item)
                        nc.vector.tensor_copy(qs[:, :], aux[aux_bank(ahead, item)][:, 0:1]).then_inc(S["dve_aux"], 1)
                    elif kind == "U":
                        c0, c1 = turned(j)
                        need_item(dve, "t_hi", b, ahead, ("T", j))
                        nc.vector.tensor_tensor(mt_lo[:, c0:c1], aux[aux_bank(ahead, ("T", j))][:, 0:c1 - c0],
                                                mt_hi[:, c0:c1].bitcast(F32), ALU.subtract).then_inc(S["dve_aux"], 1)
                    elif kind == "Q":
                        h, s = item[2], j % 2
                        if h == 0:
                            need_item(dve, "act_aux", b, ahead, ("G", j // 2))
                            if order is not FIRST:
                                need(dve, "s_full", b, NT, (ahead * PAIRS + j - 1) * KT)
                            if order is not FIRST or j:
                                before = (ahead, j - 1) if j else (0, PAIRS - 1)
                                need_item(dve, "dve_aux", b, before[0], ("M", before[1], 1, 1, NCH - 1))
                        src = qf[h * HD:(h + 1) * HD, j, :]
                        cols = slice(h * TOK, (h + 1) * TOK)
                        nc.vector.tensor_copy(qh[0:HD, s, cols], src)
                        nc.vector.tensor_copy(qh[HD:P, s, cols], src)
                        nc.vector.tensor_copy(qm[0:HD, cols], src).then_inc(S["q_hi"], 1)
                    elif kind == "P":
                        h, s = item[2], j % 2
                        need_item(dve, "q_hi", b, ahead, ("Q", j, h))
                        part = slice(h * HD, (h + 1) * HD)
                        cols = slice(h * TOK, (h + 1) * TOK)
                        nc.vector.tensor_tensor(ql[0:HD, s, cols], qf[part, j, :], qh[part, s, cols].bitcast(F32),
                                                ALU.subtract).then_inc(S["q_lo"], 1)
                    elif kind == "L":
                        c0, c1 = CHUNKS[item[2]]
                        keys = ("K",) + item[1:]
                        bank, s = aux[aux_bank(ahead, keys)], j % 2
                        for h in range(2):
                            need_item(dve, "k_hi", b, ahead, keys, 1 - h)
                            last = nc.vector.tensor_tensor(kk[HD:P, 0, s, h, c0:c1], bank[h * HD:(h + 1) * HD, 0:c1 - c0],
                                                           kk[0:HD, 0, s, h, c0:c1].bitcast(F32), ALU.subtract)
                        last.then_inc(S["dve_aux"], 1)
                    elif kind == "M":
                        h, t, c = item[2:]
                        c0, c1 = CHUNKS[c]
                        need_item(dve, "aux_full", b, ahead, item)
                        nc.vector.reduce_max(mx[:, 2 * h + t, c:c + 1], aux[aux_bank(ahead, item)][:, 0:c1 - c0],
                                             axis=AX.X).then_inc(S["dve_aux"], 1)
                    elif kind == "N":
                        need_item(dve, "dve_aux", b, ahead, ("M", j, 1, 1, NCH - 1))
                        nc.vector.tensor_reduce(m4[:, :], mx[:, :, :], axis=AX.X, op=ALU.max).then_inc(S["m4_ready"], 1)
                        need_item(dve, "m4_ready", b, ahead, item)
                        nc.vector.tensor_scalar(negm[:, :], m4[:, :], -1.0, None, ALU.mult).then_inc(S["negm_ready"], 1)
                    elif kind == "E":
                        i, w = item[2], TOK // RECIPROCAL_PARTS
                        if i == 0:
                            need(dve, "norm_done", b, PAIRS, j)
                            need(dve, "den_full", b, PAIRS, j + 1)
                        nc.vector.reciprocal(rec[:, i * w:(i + 1) * w], o_bank[j % 2][:, TOK + i * w:TOK + (i + 1) * w])\
                            .then_inc(S["rec_ready"], 1)
                    elif kind == "F":
                        need(dve, "rec_ready", b, PAIRS * RECIPROCAL_PARTS, (j + 1) * RECIPROCAL_PARTS)
                        nc.vector.tensor_tensor(ot[:, j, :], o_bank[j % 2][:, 0:TOK], rec[:, :], ALU.mult)\
                            .then_inc(S["norm_done"], 1)
                    elif kind == "H":
                        need(dve, "attn_proj", b, 1, 1)
                        for t in range(QT):
                            last = nc.vector.scalar_tensor_tensor(
                                xs[:, b, t, :], o_bank[1][:, t * DIM:(t + 1) * DIM], gates[:, 0:1],
                                xs[:, b, t, :], ALU.mult, ALU.add)
                        last.then_inc(S["x1_ready"], 1)
                assert steps[0] in (0, DVE_STEPS), steps[0]

            attention(-1, FIRST)
            dve.wait_ge(S["x_in"], 16 * (BATCH - 1))
            dve.wait_ge(S["gates_ready"], 1)
            with dve.Fori(0, BATCH - 1) as b:
                attention(b, BODY)
            attention(BATCH - 1, LAST)

            need(dve, "x1_ready", BATCH, 1, 0)
            for lane in range(LANES):
                nc.vector.memset(mts_hi[lane][:, KEYS:KPAD].bitcast(F32), 0.0)
                nc.vector.memset(mts_lo[lane][:, KEYS:KPAD].bitcast(F32), 0.0).then_inc(S["pad_ready", lane], 1)
            with dve.Fori(0, BATCH // LANES) as it:
                steps[0] = 0

                def step(instruction):
                    steps[0] += 1
                    instruction.then_inc(S["tail_step"], 1)
                    dve.wait_ge(S["tail_step"], it * TAIL_STEPS + steps[0])

                for lane in range(LANES):
                    for t in range(QT):
                        last = nc.vector.bn_stats(stat[:, lane, t, :], xs[:, it * LANES + lane, t, :])
                    step(last)
                    nc.vector.memset(var[:, lane, :], 0.0)
                    for t in range(QT):
                        last = nc.vector.bn_aggr(mv[:, lane, t, :], stat[:, lane, t, :])
                    step(last)
                    nc.vector.tensor_scalar(var[:, lane, :], mv[:, lane, :, 1], LN_EPS, None, ALU.add)\
                        .then_inc(S["var_ready", lane], 1)
                for lane in range(LANES):
                    need(dve, ("rstd_ready", lane), it, 1, 1)
                    for t in range(QT):
                        last = nc.vector.tensor_scalar(zs[lane][:, t, :], xs[:, it * LANES + lane, t, :],
                                                       mv[:, lane, t, 0:1], rstd[:, lane, t:t + 1],
                                                       ALU.subtract, ALU.mult)
                    last.then_inc(S["z_ready", lane], 1)
                for half, (c0, c1) in enumerate(((0, 1024), (1024, KEYS))):
                    for lane in range(LANES):
                        need(dve, ("media_hi", lane), it, 2, half + 1)
                        nc.vector.tensor_tensor(mts_lo[lane][:, c0:c1], lane_psum[lane][:, c0:c1],
                                                mts_hi[lane][:, c0:c1].bitcast(F32), ALU.subtract)\
                            .then_inc(S["media_lo", lane], 1)
                for lane in range(LANES):
                    for t in range(QT):
                        need(dve, ("ff2_psum", lane), it, QT, t + 1)
                        last = nc.vector.scalar_tensor_tensor(
                            x2s[lane][:, t, :], lane_bank[lane][t][:, 0:DIM], gates[:, 1:2],
                            xs[:, it * LANES + lane, t, :], ALU.mult, ALU.add)
                    last.then_inc(S["x2_ready", lane], 1)
                for lane in range(LANES):
                    need(dve, ("gm_hi_ready", lane), it, 1, 1)
                    nc.vector.scalar_tensor_tensor(gms_lo[lane][:, :], lane_bank[lane][3][:, 0:TOK], L1_SCALE,
                                                   gms_hi[lane][:, :].bitcast(F32), ALU.mult, ALU.subtract)\
                        .then_inc(S["gm_lo_ready", lane], 1)
                for t in range(QT):
                    for lane in range(LANES):
                        for half, (c0, c1) in enumerate(((0, 1024), (1024, KEYS))):
                            need(dve, ("l1_scores", lane), it, 2 * QT, 2 * t + half + 1)
                            last = nc.vector.reduce_max(l1top[lane][:, half:half + 1], lane_psum[lane][:, c0:c1], axis=AX.X)
                        step(last)
                        nc.vector.tensor_scalar(l1max[lane][:, t:t + 1], l1top[lane][:, 0:1], l1top[lane][:, 1:2], -1.0,
                                                ALU.max, ALU.mult).then_inc(S["l1_max", lane], 1)
                for lane in range(LANES):
                    for u in range(1, GROUPS, 2):
                        need(dve, ("pt_psum", lane), it, GROUPS, u + 1)
                        nc.vector.tensor_copy(pts[lane][:, 2 * u:2 * u + 2, :],
                                              lane_bank[lane][u % 4].rearrange("p (t q) -> p t q", t=2))\
                            .then_inc(S["pt_dve", lane], 1)
                for lane in range(LANES):
                    need(dve, ("l1_exp", lane), it, QT, QT)
                    step(nc.vector.reciprocal(l1rec[lane][:, :], l1den[lane][:, :]))
                    need(dve, ("ctx_psum", lane), it, 1, 1)
                    for t in range(QT):
                        last = nc.vector.tensor_scalar(cxs[lane][:, t, :], lane_bank[lane][1][:, t * DIM:(t + 1) * DIM],
                                                       l1rec[lane][:, t:t + 1], None, ALU.mult)
                    last.then_inc(S["ctx_ready", lane], 1)
                for lane in range(LANES):
                    gate, fused = gate_s[lane][:, :, :], fuseds[lane][:, :, :]
                    need(dve, ("gate_ready", lane), it, 1, 1)
                    step(nc.vector.tensor_scalar(gate, gate, 0.5, 0.5, ALU.mult, ALU.add))
                    step(nc.vector.tensor_tensor(fused, gate, cxs[lane][:, :, :], ALU.mult))
                    nc.vector.tensor_tensor(fused, fused, x2s[lane][:, :, :], ALU.add).then_inc(S["fused_ready", lane], 1)
                for lane in range(LANES):
                    need(dve, ("square_ready", lane), it, 1, 1)
                    nc.vector.tensor_scalar(var[:, lane, :], l1sum[lane][:, :], 1.0 / DIM, RMS_EPS, ALU.mult, ALU.add)\
                        .then_inc(S["ssq_ready", lane], 1)
                for lane in range(LANES):
                    need(dve, ("rms_ready", lane), it, 1, 1)
                    if lane == 0:
                        dve.wait_ge(S["late_weights_in"], 16 * 3)
                    need(dve, ("out_stored", lane), it, 16, 0)
                    for t in range(QT):
                        nc.vector.scalar_tensor_tensor(ress[lane][:, t, :], fuseds[lane][:, t, :],
                                                       rstd[:, lane, t:t + 1], normw[:, :],
                                                       ALU.mult, ALU.mult).then_inc(S["out_ready", lane], 1)
            assert steps[0] == TAIL_STEPS, steps[0]

        @block.tensor
        def _(pe):
            mm = nc.tensor.matmul
            pe.wait_ge(S["identity"], 3)

            def transpose_tokens(dst, src):
                for t in range(DT):
                    for q in range(QT):
                        last = nc.tensor.transpose(dst[:, t * TOK + q * P:t * TOK + (q + 1) * P],
                                                   src[:, q, t * P:(t + 1) * P], ident[:, :])
                return last

            def attention(b, order):
                for ahead, item in order:
                    kind, j = item[0], None if len(item) == 1 else item[1]
                    if order is FIRST and item == ("K", 0, 0):
                        pe.wait_ge(S["kv_split"], 2)
                    if order is FIRST and item == ("W", 0):
                        pe.wait_ge(S["norms_in"], 16 * 4)
                        nc.tensor.transpose(o_bank[1][:, 0:4 * DT], normrows[:, :], ident[0:4 * DT, 0:4 * DT])\
                            .then_inc(S["norms_psum"], 1)
                    if order is FIRST and item == ("G", 0):
                        pe.wait_ge(S["wq_in"], 16)
                    if kind in COUNTED["aux_full"]:
                        bank = aux[aux_bank(ahead, item)]
                        if (order is FIRST, (ahead, item)) in AUX_BEFORE:
                            emptied(pe, b, *AUX_BEFORE[order is FIRST, (ahead, item)])
                    if kind == "T":
                        if j == 0:
                            need(pe, "media_in", b, 32, 64)
                        for i, t in enumerate(range(TURN * j, min(TURN * (j + 1), KT))):
                            r = rows_of(t)
                            last = nc.tensor.transpose(bank[:, i * P:i * P + r], nat0[0:r, t, :], ident[0:r, 0:r])
                        last.then_inc(S["aux_full"], 1)
                    elif kind == "W":
                        need(pe, "z_ready", b, 1, 2)
                        for q in range(QT):
                            last = nc.tensor.transpose(bank[:, q * P:(q + 1) * P], z[:, q, j * P:(j + 1) * P], ident[:, :])
                        last.then_inc(S["aux_full"], 1)
                    elif kind == "C":
                        need(pe, "q_scale_ready", b, 1, 2)
                        mm(bank[:, 0:1], ones[MASK_ROW:MASK_ROW + 1, :], msum[MASK_ROW:MASK_ROW + 1, 2:3],
                           start=True, stop=True).then_inc(S["aux_full"], 1)
                    elif kind == "G":
                        need_item(pe, "act_aux", b, ahead, ("W", DT - 1))
                        for i in range(2):
                            c0 = (2 * j + i) * P
                            for t in range(DT):
                                last = mm(bank[:, i * TOK:(i + 1) * TOK], wq[:, t, c0:c0 + P], zt[:, t, :],
                                          start=(t == 0), stop=(t == DT - 1))
                        last.then_inc(S["aux_full"], 1)
                    elif kind == "K":
                        if j == 0 and item[2] == 0:
                            need_item(pe, "dve_aux", b, ahead, ("U", TUNITS - 1))
                        c0, c1 = CHUNKS[item[2]]
                        w = slice(j * P, (j + 1) * P)
                        split_mm(bank[:, 0:c1 - c0], [(wk_hi[:, w], mt_hi[:, c0:c1]), (wk_hi[:, w], mt_lo[:, c0:c1]),
                                                      (wk_lo[:, w], mt_hi[:, c0:c1])]).then_inc(S["aux_full"], 1)
                    elif kind == "V":
                        w = slice(j * 256, (j + 1) * 256)
                        for i, t in enumerate(range(2 * item[2], min(2 * item[2] + 2, KT))):
                            r = rows_of(t)
                            k = slice(t * P, t * P + r)
                            last = split_mm(bank[0:r, i * 256:(i + 1) * 256],
                                            [(mt_hi[:, k], wv_hi[:, w]), (mt_hi[:, k], wv_lo[:, w]),
                                             (mt_lo[:, k], wv_hi[:, w])])
                        last.then_inc(S["aux_full"], 1)
                    elif kind == "M":
                        h, t, c = item[2:]
                        c0, c1 = CHUNKS[c]
                        if h == 0 and t == 0:
                            need_item(pe, "k_hi", b, ahead, ("K", j, c))
                            if c == 0:
                                need_item(pe, "q_hi", b, ahead, ("Q", j, 1))
                                if j < 2:
                                    need(pe, f"mask_rows{j}", b, 16 * (j + 1), 16 * (j + 1) * (1 + ahead))
                        q0 = h * TOK + t * P
                        mm(bank[:, 0:c1 - c0], qm[:, q0:q0 + P], kk[0:KX, 1, j % 2, h, c0:c1],
                           start=True, stop=True).then_inc(S["aux_full"], 1)
                    elif kind == "R":
                        need_item(pe, "negm_ready", b, ahead, ("N", j))
                        for i in range(4):
                            last = mm(bank[ONE_ROW:ONE_ROW + 1, i * P:(i + 1) * P], negm[:, i:i + 1], ident[:, :],
                                      start=True, stop=True)
                        last.then_inc(S["aux_full"], 1)
                    elif kind == "S":
                        t, s = item[2], j % 2
                        m = (ahead * PAIRS + j) * KT + t
                        if t == 0:
                            need_item(pe, "dve_aux", b, ahead, ("L", j, NCH - 1))
                            need_item(pe, "act_aux", b, ahead, ("R", j))
                            need_item(pe, "q_lo", b, ahead, ("P", j, 1))
                        need(pe, "p_ready", b, NT, m - SBANKS + 1)
                        r = rows_of(t)
                        k = slice(t * P, t * P + r)
                        for h in range(2):
                            q = slice(h * TOK, (h + 1) * TOK)
                            dst = score_bank[m % SBANKS][0:r, q]
                            mm(dst, kk[:, 0, s, h, k], qh[:, s, q], start=True, stop=False)
                            last = mm(dst, kk[0:KX, 1, s, h, k], ql[:, s, q], start=False, stop=True)
                        last.then_inc(S["s_full"], 1)
                    elif kind == "A":
                        t, s = item[2], j % 2
                        g, i = divmod(t, 2)
                        jj = ahead * PAIRS + j
                        n = jj * GROUPS + g
                        need(pe, "p_ready", b, NT, jj * KT + t + 1)
                        if t == 0:
                            if j == 1:
                                need(pe, "x1_ready", b, 1, ahead)
                            else:
                                need(pe, "norm_done", b, PAIRS, jj - 1)
                            need_item(pe, "act_aux", b, ahead, ("V", j // 2, GROUPS - 1))
                        r = rows_of(t)
                        for h in range(2):
                            d0 = (j % 2) * P + h * HD
                            last = mm(o_bank[s][h * HD:(h + 1) * HD, 0:TOK], v[0:r, (j // 2) % 2, t, d0:d0 + HD],
                                      pe_ring[0:r, n % PRING, i * 512 + h * TOK:i * 512 + (h + 1) * TOK],
                                      start=(t == 0), stop=(t == KT - 1))
                        if i == 1 or t == KT - 1:
                            last.then_inc(S["av_done"], 1)
                    elif kind == "D":
                        if order is LAST and j == PAIRS - 1:
                            pe.wait_ge(S["gate_weights_in"], 16 * 3)
                            for f in range(2 * DT):
                                for t in range(DT):
                                    nc.tensor.transpose(wide[:, f * DIM + t * P:f * DIM + (t + 1) * P],
                                                        raw_wg[:, t, f * P:(f + 1) * P], ident[:, :])
                            for t in range(DT):
                                last = nc.tensor.transpose(side[0][:, t * P:(t + 1) * P], wm[:, t, :], ident[:, :])
                            last.then_inc(S["wmt_psum"], 1)
                        need(pe, "acc_done", b, NG, (j + 1) * GROUPS)
                        for h in range(2):
                            last = mm(o_bank[j % 2][h * HD:(h + 1) * HD, TOK:2 * TOK], ones[:, 0:HD],
                                      acc[:, h * TOK:(h + 1) * TOK], start=True, stop=True)
                        last.then_inc(S["den_full"], 1)
                    elif kind == "O":
                        t, part = item[1:]
                        if t == 0 and part == 0:
                            need(pe, "norm_done", b, PAIRS, PAIRS)
                        for i in range(part * PAIRS // 2, (part + 1) * PAIRS // 2):
                            last = mm(o_bank[1][:, t * DIM:(t + 1) * DIM], ot[:, i, t * P:(t + 1) * P], wo[:, i, :],
                                      start=(i == 0), stop=(i == PAIRS - 1))
                        if t == QT - 1 and part == 1:
                            last.then_inc(S["attn_proj"], 1)

            attention(-1, FIRST)
            pe.wait_ge(S["weights_in"], 16 * 3)
            with pe.Fori(0, BATCH - 1) as b:
                attention(b, BODY)
            attention(BATCH - 1, LAST)
            pe.wait_ge(S["wmt_ready"], 1)
            need(pe, "x1_ready", BATCH, 1, 0)

            with pe.Fori(0, BATCH // LANES) as it:
                for lane in range(LANES):
                    need(pe, ("gate_ready", lane), it, 1, 0)
                    need(pe, ("media_in", lane), it, 32, 32)
                    for t in range(KT):
                        r = rows_of(t)
                        last = nc.tensor.transpose(lane_psum[lane][:, t * P:t * P + r], nats[lane][0:r, t, :],
                                                   ident[0:r, 0:r])
                        if t in (7, KT - 1):
                            last.then_inc(S["media_t_psum", lane], 1)
                for lane in range(LANES):
                    need(pe, ("z_ready", lane), it, 1, 1)
                    need(pe, ("media_lo", lane), it, 2, 1)
                    transpose_tokens(lane_bank[lane][0], zs[lane]).then_inc(S["zt_psum", lane], 1)
                pe.wait_ge(S["late_weights_in"], 16 * 3)
                for lane in range(LANES):
                    need(pe, ("zt_ready", lane), it, 1, 1)
                    for f in range(FT):
                        if f == FT // 2:
                            need(pe, ("media_lo", lane), it, 2, 2)
                        for t in range(DT):
                            last = mm(lane_psum[lane][:, f * TOK:(f + 1) * TOK], w1[:, t, f * P:(f + 1) * P],
                                      zts[lane][:, t, :], start=(t == 0), stop=(t == DT - 1))
                        if f % 4 == 3:
                            last.then_inc(S["ff1_psum", lane], 1)
                for lane in range(LANES):
                    for t in range(QT):
                        for f in range(FT):
                            if t == 0 and f % 4 == 0:
                                need(pe, ("gelu_ready", lane), it, 2, f // 4 + 1)
                            last = mm(lane_bank[lane][t][:, 0:DIM], gts[lane][:, f, t * P:(t + 1) * P],
                                      w2[:, f, :], start=(f == 0), stop=(f == FT - 1))
                        last.then_inc(S["ff2_psum", lane], 1)
                for lane in range(LANES):
                    need(pe, ("x2_ready", lane), it, 1, 1)
                    transpose_tokens(lane_bank[lane][2], x2s[lane]).then_inc(S["x2t_psum", lane], 1)
                for lane in range(LANES):
                    need(pe, ("x2t_ready", lane), it, 1, 1)
                    for t in range(DT):
                        last = mm(lane_bank[lane][3][:, 0:TOK], wm[:, t, :], zts[lane][:, t, :],
                                  start=(t == 0), stop=(t == DT - 1))
                    last.then_inc(S["gm_psum", lane], 1)
                for t in range(QT):
                    for lane in range(LANES):
                        need(pe, *((("l1_exp", lane), it, QT, t) if t else (("gm_lo_ready", lane), it, 1, 1)))
                        if t == 0:
                            pe.wait_ge(S["pad_ready", lane], 1)
                        q = slice(t * P, (t + 1) * P)
                        hi, lo = mts_hi[lane], mts_lo[lane]
                        for c0 in range(0, KPAD, 512):
                            c1 = min(c0 + 512, KPAD)
                            last = split_mm(lane_psum[lane][:, c0:c1], [(gms_hi[lane][:, q], hi[:, c0:c1]),
                                                                        (gms_hi[lane][:, q], lo[:, c0:c1]),
                                                                        (gms_lo[lane][:, q], hi[:, c0:c1])])
                            if c1 in (1024, KPAD):
                                last.then_inc(S["l1_scores", lane], 1)
                for lane in range(LANES):
                    need(pe, ("l1_exp", lane), it, QT, QT)
                    for u in range(GROUPS):
                        if u >= 4:
                            w = u - 4
                            need(pe, *((("pt_dve", lane), it, GROUPS // 2) if w % 2 else
                                       (("pt_act", lane), it, GROUPS // 2 + 1)), w // 2 + 1)
                        for i, t in enumerate(range(2 * u, min(2 * u + 2, KT))):
                            r = rows_of(t)
                            for q in range(QT):
                                c0 = i * TOK + q * P
                                last = nc.tensor.transpose(lane_bank[lane][u % 4][0:r, c0:c0 + P],
                                                           p1s[lane][:, q, t * P:t * P + r], ident[:, :])
                        last.then_inc(S["pt_psum", lane], 1)
                for lane in range(LANES):
                    need(pe, ("pt_act", lane), it, GROUPS // 2 + 1, GROUPS // 2 + 1)
                    need(pe, ("pt_dve", lane), it, GROUPS // 2, GROUPS // 2)
                    for t in range(KT):
                        r = rows_of(t)
                        last = mm(lane_bank[lane][3][:, 0:TOK], nats[lane][0:r, t, :], pts[lane][0:r, t, :],
                                  start=(t == 0), stop=(t == KT - 1))
                    last.then_inc(S["u_psum", lane], 1)
                for lane in range(LANES):
                    need(pe, ("u_ready", lane), it, 1, 1)
                    for q in range(QT):
                        last = mm(lane_bank[lane][1][:, q * DIM:(q + 1) * DIM], uts[lane][:, q * P:(q + 1) * P],
                                  wmt[:, :], start=True, stop=True)
                    last.then_inc(S["ctx_psum", lane], 1)
                for lane in range(LANES):
                    need(pe, ("ctx_ready", lane), it, 1, 1)
                    transpose_tokens(lane_bank[lane][2], cxs[lane]).then_inc(S["ct_psum", lane], 1)
                for lane in range(LANES):
                    need(pe, ("ct_ready", lane), it, 1, 1)
                    for q in range(QT):
                        dst = lane_bank[lane][3][:, q * DIM:(q + 1) * DIM]
                        for t in range(DT):
                            mm(dst, zts[lane][:, t, q * P:(q + 1) * P], wg[:, t, :], start=(t == 0), stop=False)
                        for t in range(DT):
                            mm(dst, cts[lane][:, t, q * P:(q + 1) * P], wg[:, DT + t, :], start=False, stop=False)
                        last = mm(dst, ones[0:1, :], bgate[:, :], start=False, stop=True)
                    last.then_inc(S["gate_psum", lane], 1)


_INS = ['x', 'ctx_1024', 'mask_BxS2_bk0', 'L0_xattn_ln_q_g', 'L0_xattn_ln_q_b', 'L0_xattn_Wq', 'L0_xattn_Wkv',
        'L0_xattn_Wo', 'L0_xattn_attn_gate', 'L0_xattn_ln_ff_g', 'L0_xattn_ln_ff_b', 'L0_xattn_W1', 'L0_xattn_W2',
        'L0_xattn_ff_gate', 'L1_xattn_W_mem', 'L1_xattn_W_gate', 'L1_xattn_b_gate', 'L1_xattn_norm_w']


def kernel(**inputs):
    import numpy as _np
    import concourse.bacc as _bacc
    from concourse import mybir as _mybir
    from concourse.bass_utils import run_bass_kernel_spmd as _run

    nc = _bacc.Bacc("TRN2", target_bir_lowering=False, num_devices=1)
    arrays, args = {}, []
    for name in _INS:
        a = _np.ascontiguousarray(inputs[name])
        arrays[f"in_{name}_dram"] = a
        args.append(nc.dram_tensor(f"in_{name}_dram", a.shape, _mybir.dt.from_np(a.dtype), kind="ExternalInput").ap())
    shape = inputs['x'].shape
    args.append(nc.dram_tensor("out_0_dram", shape, _mybir.dt.float32, kind="ExternalOutput").ap())
    cross_attention_kernel(nc, *args)
    r = _run(nc, [arrays], core_ids=[0])
    return r.results[0]["out_0_dram"]
```
